# Optimizing a Trainium2 kernel written in Bass

```python
import numpy as np
import jax
import jax.numpy as jnp

def _softmax(x, axis=-1):
    return jax.nn.softmax(x, axis=axis)
def _gelu(x):
    return jax.nn.gelu(x, approximate=True)
def _silu(x):
    return jax.nn.silu(x)
def _sigmoid(x):
    return jax.nn.sigmoid(x)
def _layernorm(x, axis=-1, eps=1e-5):
    m = jnp.mean(x, axis=axis, keepdims=True)
    v = jnp.var(x, axis=axis, keepdims=True)
    return (x - m) / jnp.sqrt(v + eps)
def _scatter_add(tgt, idx, src, axis=0):
    return tgt.at[idx].add(src)
def _segment_sum(src, seg, n):
    return jax.ops.segment_sum(src, seg, n)

kernel_name = 'mk_conv_seq_d2_conv_nchw512_606141'

def setup_inputs(seed: int = 0):
    np.random.seed(seed)
    _w = jnp.asarray
    def _rec_inputs():
        import jax
        import jax.numpy as jnp
        _gk = jax.random.key(seed)
        x = 7.22e-05 + 1 * jax.random.normal(jax.random.fold_in(_gk, 1), (16, 512, 32, 32), jnp.float32)
        return x
    x = _rec_inputs()
    def _L0_conv_setup():
        import jax, jax.numpy as jnp
        import numpy as np
        N_HEADS = 8
        D_K = 64
        SCALE = D_K ** (-0.5)
        key = jax.random.key(seed)
        k1, k2, k3, k4, k5 = jax.random.split(key, 5)
        C = 512
        inner = N_HEADS * D_K
        return {'x': jax.random.normal(k1, (16, C, 32, 32), dtype=jnp.float32), 'W_qkv': jax.random.normal(k2, (C, 3 * inner), dtype=jnp.float32) * C ** (-0.5), 'b_qkv': jax.random.normal(k3, (3 * inner,), dtype=jnp.float32) * 0.02, 'W_out': jax.random.normal(k4, (inner, C), dtype=jnp.float32) * inner ** (-0.5), 'b_out': jax.random.normal(k5, (C,), dtype=jnp.float32) * 0.02}
    _L0_conv_all = _L0_conv_setup()
    _L0_conv_in = {k: v for k, v in _L0_conv_all.items() if k in ('W_qkv', 'b_qkv', 'W_out', 'b_out', )}
    del _L0_conv_all

    def _L1_conv_setup():
        import jax, jax.numpy as jnp
        import numpy as np
        BN_EPS = 1e-05

        def relu6(v):
            return jnp.clip(v, 0.0, 6.0)
        key = jax.random.key(seed)
        ks = jax.random.split(key, 7)
        C, R = (512, 128)
        B, H, W = (8, 128, 128)
        x = jax.random.normal(ks[0], (B, C, H, W), dtype=jnp.float32)
        w_guide = jax.random.normal(ks[1], (R, C), dtype=jnp.float32) * (1.0 / np.sqrt(C))
        w_fuse = jax.random.normal(ks[2], (C, R), dtype=jnp.float32) * (1.0 / np.sqrt(R))
        bn_gamma = jax.random.normal(ks[3], (C,), dtype=jnp.float32) * 0.1 + 1.0
        bn_beta = jax.random.normal(ks[4], (C,), dtype=jnp.float32) * 0.1
        bn_mean = jax.random.normal(ks[5], (C,), dtype=jnp.float32) * 0.1
        bn_var = jax.random.uniform(ks[6], (C,), dtype=jnp.float32, minval=0.5, maxval=1.5)
        return {'x': x, 'w_guide': w_guide, 'w_fuse': w_fuse, 'bn_gamma': bn_gamma, 'bn_beta': bn_beta, 'bn_mean': bn_mean, 'bn_var': bn_var}
    _L1_conv_all = _L1_conv_setup()
    _L1_conv_in = {k: v for k, v in _L1_conv_all.items() if k in ('w_guide', 'w_fuse', 'bn_gamma', 'bn_beta', 'bn_mean', 'bn_var', )}
    del _L1_conv_all

    return {
        "x": x,
        "L0_conv_W_qkv": _L0_conv_in["W_qkv"],
        "L0_conv_b_qkv": _L0_conv_in["b_qkv"],
        "L0_conv_W_out": _L0_conv_in["W_out"],
        "L0_conv_b_out": _L0_conv_in["b_out"],
        "L1_conv_w_guide": _L1_conv_in["w_guide"],
        "L1_conv_w_fuse": _L1_conv_in["w_fuse"],
        "L1_conv_bn_gamma": _L1_conv_in["bn_gamma"],
        "L1_conv_bn_beta": _L1_conv_in["bn_beta"],
        "L1_conv_bn_mean": _L1_conv_in["bn_mean"],
        "L1_conv_bn_var": _L1_conv_in["bn_var"],
    }

def reference(x, L0_conv_W_qkv, L0_conv_b_qkv, L0_conv_W_out, L0_conv_b_out, L1_conv_w_guide, L1_conv_w_fuse, L1_conv_bn_gamma, L1_conv_bn_beta, L1_conv_bn_mean, L1_conv_bn_var):
    import jax
    import jax.numpy as jnp
    def _L0_conv_ref(x, W_qkv, b_qkv, W_out, b_out):
        import jax, jax.numpy as jnp
        import numpy as np
        N_HEADS = 8
        D_K = 64
        SCALE = D_K ** (-0.5)
        B, C, H, W = x.shape
        N = H * W
        xt = x.reshape(B, C, N).transpose(0, 2, 1)
        qkv = (xt @ W_qkv + b_qkv).reshape(B, N, N_HEADS, 3 * D_K)
        q, k, v = jnp.split(qkv, 3, axis=-1)
        attn = jnp.einsum('bihd,bjhd->bhij', q, k) * SCALE
        attn = jax.nn.softmax(attn, axis=-1)
        res = jnp.einsum('bhij,bjhd->bihd', attn, v).reshape(B, N, N_HEADS * D_K)
        res = res @ W_out + b_out + xt
        return res.transpose(0, 2, 1).reshape(B, C, H, W)

    def _L1_conv_ref(x, w_guide, w_fuse, bn_gamma, bn_beta, bn_mean, bn_var):
        import jax, jax.numpy as jnp
        import numpy as np
        BN_EPS = 1e-05

        def relu6(v):
            return jnp.clip(v, 0.0, 6.0)
        y = jnp.mean(x, axis=(2, 3))
        y = relu6(jnp.einsum('rc,bc->br', w_guide, y))
        y = jnp.einsum('cr,br->bc', w_fuse, y)
        inv_std = jax.lax.rsqrt(bn_var + BN_EPS)
        y = relu6((y - bn_mean) * inv_std * bn_gamma + bn_beta)
        return x + y[:, :, None, None]

    def _gn(v, G=32, eps=1e-5):
        B_, C_, H_, W_ = v.shape
        g = v.reshape(B_, G, C_ // G, H_, W_)
        m = jnp.mean(g, axis=(2, 3, 4), keepdims=True)
        s = jnp.var(g, axis=(2, 3, 4), keepdims=True)
        return ((g - m) / jnp.sqrt(s + eps)).reshape(v.shape)

    def _ln_c(v, eps=1e-6):
        m = jnp.mean(v, axis=1, keepdims=True)
        s = jnp.var(v, axis=1, keepdims=True)
        return (v - m) / jnp.sqrt(s + eps)

    def _ln_t(v, eps=1e-5):
        m = jnp.mean(v, axis=-1, keepdims=True)
        s = jnp.var(v, axis=-1, keepdims=True)
        return (v - m) / jnp.sqrt(s + eps)

    def _to_tokens(v):
        B_, C_, H_, W_ = v.shape
        return v.reshape(B_, C_, H_ * W_).transpose(0, 2, 1)
    def _from_tokens(t, like):
        B_, C_, H_, W_ = like.shape
        return t.transpose(0, 2, 1).reshape(B_, C_, H_, W_)

    x = _L0_conv_ref(x, L0_conv_W_qkv, L0_conv_b_qkv, L0_conv_W_out, L0_conv_b_out)
    x = _L1_conv_ref(x, L1_conv_w_guide, L1_conv_w_fuse, L1_conv_bn_gamma, L1_conv_bn_beta, L1_conv_bn_mean, L1_conv_bn_var)
    return x


_drawn_inputs = setup_inputs


def setup_inputs(seed=0):
    import zlib

    import numpy as np

    out = dict(_drawn_inputs(seed))
    spreads = {}
    factors = {'L1_conv_bn_gamma': 7.99, 'L1_conv_bn_var': 4.537}
    for name, (base, spread) in spreads.items():
        noise = np.random.default_rng([zlib.crc32(name.encode()), seed]).standard_normal(out[name].shape)
        drawn = base * np.exp(spread * noise) if base else spread * noise
        out[name] = jnp.asarray(drawn.astype(out[name].dtype))
    for name, factor in factors.items():
        out[name] = (out[name] * factor).astype(out[name].dtype)
    return out
```

```python
from contextlib import ExitStack

import concourse.bass as bass
from concourse import mybir

P = 128
F32 = mybir.dt.float32
F32R = mybir.dt.float32r
ALU = mybir.AluOpType
ACT = mybir.ActivationFunctionType
AX_X = mybir.AxisListType.X

BATCH, C, TOK = 16, 512, 1024
HEADS, DK, RED = 8, 64, 128
CK = C // P
HALF = TOK // 2
KT = TOK // P
PAIRS = HEADS // 2
UNITS = 2 * KT
STEPS = HEADS * UNITS
QKV = 3 * DK
VW = DK + 1
LAG = 2
SCORE_BANKS, HI_BUFS, LO_BUFS, RAW_BUFS = 3, 3, 2, 2
SCALE = DK ** -0.5
BN_EPS = 1e-5

QK_AT = {0: 0, 3: 1}
MAX_AT = {6: 0, 7: 1, 8: 2, 9: 3, 11: 4, 12: 5, 13: 6, 14: 7}
SHIFT1_AT, SHIFT0_AT = 1, 11
OUT_AT = {4: (0, 0), 5: (0, 1), 6: (0, 2), 7: (0, 3), 12: (1, 0), 13: (1, 1), 14: (1, 2), 15: (1, 3)}
POOL_LO = (7, 9, 12, 14)
DEN_AT, RCP_AT, NORM_AT, RES_AT = (10, 2), (12, 4), (15, 7), (0, 8)
X_AT = {6: (5, 8, 11, 14), 7: (1, 4, 7, 10)}

SEAM = [("qk", 0), ("v", 0), ("qk", 1), ("v", 1), ("out", 0, 0), ("v", 2), ("out", 0, 1), ("max", 0),
        ("v", 3), ("out", 0, 2), ("out", 0, 3), ("max", 1), ("v", 4), ("out", 1, 0), ("max", 2),
        ("out", 1, 1), ("v", 5), ("out", 1, 2), ("max", 3), ("out", 1, 3), ("v", 6), ("max", 4),
        ("gate1",), ("v", 7), ("max", 5), ("gate2",), ("max", 6), ("shift",), ("max", 7)]


def seam(ends, begins):
    return [i for i in SEAM if (ends if i[0] in ("out", "gate1", "gate2") else begins)]


def beside(h, u):
    items = []
    if u in QK_AT and h + 1 < HEADS:
        items.append(("qk", h + 1, QK_AT[u]))
    if u == SHIFT1_AT:
        items.append(("shift", h, 1))
    if u in OUT_AT and h % 2 == 0 and h > 0:
        items.append(("out", h // 2 - 1, *OUT_AT[u]))
    if u in MAX_AT and h + 1 < HEADS:
        items.append(("max", h + 1, MAX_AT[u]))
    if u == SHIFT0_AT and h + 1 < HEADS:
        items.append(("shift", h + 1, 0))
    return items


def lo_done(g):
    pool = g % UNITS in POOL_LO
    return pool, sum((i % UNITS in POOL_LO) == pool for i in range(g + 1))


LO_POOL = HEADS * len(POOL_LO)
LO_DVE = STEPS - LO_POOL


def attention_block_kernel(nc, x, w_qkv, b_qkv, w_out, b_out, w_guide, w_fuse, gamma, beta, mean, var, out):
    x_v = x.rearrange("b (k p) h w -> b p k (h w)", p=P)
    out_v = out.rearrange("b (k p) h w -> b p k (h w)", p=P)
    wq_v = w_qkv.rearrange("(k p) n -> p k n", p=P)

    with ExitStack() as ctx:
        def sb(name, shape, dt=F32):
            return ctx.enter_context(nc.sbuf_tensor(name, shape, dt))

        def sem(name):
            return ctx.enter_context(nc.semaphore(name))

        wqkv_hi = sb("wqkv_hi", [P, CK, 3 * C], F32R)
        wqkv_lo = sb("wqkv_lo", [P, CK, 3 * C], F32R)
        wout_hi = sb("wout_hi", [P, PAIRS, C], F32R)
        wout_lo = sb("wout_lo", [P, PAIRS, C], F32R)
        x_hi = sb("x_hi", [P, CK, TOK], F32R)
        x_lo = sb("x_lo", [P, CK, TOK], F32R)
        x_raw = sb("x_raw", [P, HALF])
        v_hi = sb("v_hi", [P, KT, HEADS * VW], F32R)
        v_lo = sb("v_lo", [P, KT, HEADS * VW], F32R)
        q_both = sb("q_both", [P, 2, TOK], F32R)
        k_twice = sb("k_twice", [P, 2, TOK], F32R)
        k_low = sb("k_low", [P, 2, TOK], F32R)
        q_shift = sb("q_shift", [P, 2, HALF], F32R)
        p_raw = sb("p_raw", [P, RAW_BUFS, HALF])
        p_hi = sb("p_hi", [P, HI_BUFS, HALF], F32R)
        p_lo = sb("p_lo", [P, LO_BUFS, HALF], F32R)
        acc = sb("acc", [P, CK, TOK])
        res_hi = sb("res_hi", [P, TOK], F32R)
        res_lo = sb("res_lo", [P, TOK], F32R)
        den_rows = sb("den_rows", [32, HALF])
        res = sb("res", [P, 2, HALF])
        den_sp = sb("den_sp", [P, HALF // P])
        rcp_sp = sb("rcp_sp", [P, HALF // P])
        top = sb("top", [P, 2, KT])
        top_row = sb("top_row", [4, 2, P], F32R)
        ident = sb("ident", [P, P])
        guide_t = sb("guide_t", [P, CK, RED])
        fuse_t = sb("fuse_t", [P, C])
        b_qk = sb("b_qk", [P, HEADS])
        b_v = sb("b_v", [P, PAIRS])
        b_res = sb("b_res", [P, CK])
        bn = sb("bn", [P, 4, CK])
        bn_scale = sb("bn_scale", [P, CK])
        bn_shift = sb("bn_shift", [P, CK])
        tmp = sb("tmp", [P, 4, CK])
        sums = sb("sums", [P, CK, 2])
        avg = sb("avg", [P, CK])
        y1 = sb("y1", [P, 1])
        y2 = sb("y2", [P, 4, CK])
        rcp_dram = nc.dram_tensor("rcp_dram", [2, HALF], F32, kind="Internal").ap()

        ps_s = ctx.enter_context(nc.psum_tensor("ps_s", [P, SCORE_BANKS, HALF], F32))
        ps_o = ctx.enter_context(nc.psum_tensor("ps_o", [P, 2, HALF], F32))
        ps_m = ctx.enter_context(nc.psum_tensor("ps_m", [P, 2, HALF], F32))
        ps_p = ctx.enter_context(nc.psum_tensor("ps_p", [P, HALF], F32))

        w_loaded = sem("w_loaded")
        w_hi_done = sem("w_hi_done")
        w_lo_done = sem("w_lo_done")
        vec_loaded = sem("vec_loaded")
        consts_done = sem("consts_done")
        tr_ps = sem("tr_ps")
        tr_done = sem("tr_done")
        b_ps = sem("b_ps")
        b_done = sem("b_done")
        std_in = sem("std_in")
        std_done = sem("std_done")
        set_chain = sem("set_chain")
        x_loaded = sem("x_loaded")
        x_hi_done = sem("x_hi_done")
        x_lo_done = sem("x_lo_done")
        acc_loaded = sem("acc_loaded")
        qk_ps = sem("qk_ps")
        v_ps = sem("v_ps")
        max_ps = sem("max_ps")
        shift_ps = sem("shift_ps")
        score_ps = sem("score_ps")
        pv_ps = sem("pv_ps")
        out_ps = sem("out_ps")
        gate1_ps = sem("gate1_ps")
        gate2_ps = sem("gate2_ps")
        qk_hi_done = sem("qk_hi_done")
        v_hi_done = sem("v_hi_done")
        top_row_done = sem("top_row_done")
        p_hi_done = sem("p_hi_done")
        p_raw_done = sem("p_raw_done")
        den_done = sem("den_done")
        res_hi_done = sem("res_hi_done")
        y_done = sem("y_done")
        qk_lo_done = sem("qk_lo_done")
        v_lo_done = sem("v_lo_done")
        max_done = sem("max_done")
        p_lo_dve = sem("p_lo_dve")
        rcp_done = sem("rcp_done")
        norm_done = sem("norm_done")
        out_done = sem("out_done")
        avg_done = sem("avg_done")
        y1_done = sem("y1_done")
        y2_done = sem("y2_done")
        gate_chain = sem("gate_chain")
        p_lo_pool = sem("p_lo_pool")
        res_lo_done = sem("res_lo_done")
        shift_in = [sem("shift_in0"), sem("shift_in1")]
        den_spread = sem("den_spread")
        rcp_out = sem("rcp_out")
        rcp_in = sem("rcp_in")
        stored = sem("stored")

        half_cols = [slice(0, HALF), slice(HALF, TOK)]

        def rows(h):
            return slice(DK * (h % 2), DK * (h % 2) + DK)

        def last(n, m=1):
            return lambda b, i: b * (n * m) + (i + 1) * m

        n_qk = n_shift = n_head_half = last(2 * HEADS)
        n_pair_half = last(2 * PAIRS)
        n_v = last(KT)
        n_max = last(HEADS * KT)
        n_step = last(STEPS)
        n_out = last(PAIRS * 2 * CK)
        n_one = last(1)
        n_x = last(2 * CK)
        n_x_dma = last(2 * CK, 16)
        n_shift_dma = last(HEADS, 32)
        n_head_half_dma = last(2 * HEADS, 16)
        out_i = lambda p, half, m: (p * 2 + half) * CK + m

        block = ctx.enter_context(nc.Block())

        @block.sync
        def _(sp):
            flat = acc[:].rearrange("p k n -> p (k n)")
            def load_first_x(j):
                if j:
                    sp.wait_ge(x_lo_done, j)
                sp.dma_start(x_raw[:, :], x_v[0][:, j // 2, half_cols[j % 2]]).then_inc(x_loaded, 16)

            for part in range(2):
                if part:
                    sp.wait_ge(w_lo_done, 1)
                sp.dma_start(flat[:, 0:2 * 3 * C].rearrange("p (k n) -> p k n", k=2),
                             wq_v[:, 2 * part:2 * part + 2, :]).then_inc(w_loaded, 16)
                load_first_x(part)
                if part == 0:
                    sp.dma_start(bn[:, 0, :], gamma.rearrange("(k p) -> p k", p=P),
                                 allow_slow_non_contiguous=True).then_inc(vec_loaded, 16)
                    sp.dma_start(bn[:, 1, :], beta.rearrange("(k p) -> p k", p=P),
                                 allow_slow_non_contiguous=True).then_inc(vec_loaded, 16)
                    sp.dma_start(bn[:, 2, :], mean.rearrange("(k p) -> p k", p=P),
                                 allow_slow_non_contiguous=True).then_inc(vec_loaded, 16)
                    sp.dma_start(bn[:, 3, :], var.rearrange("(k p) -> p k", p=P),
                                 allow_slow_non_contiguous=True).then_inc(vec_loaded, 16)
                    sp.dma_start(tmp[:, 3, :], b_out.rearrange("(k p) -> p k", p=P),
                                 allow_slow_non_contiguous=True).then_inc(vec_loaded, 16)
                    sp.dma_start(b_qk[:, :], b_qkv.rearrange("(h j) -> j h", j=QKV)[0:P, :],
                                 allow_slow_non_contiguous=True).then_inc(vec_loaded, 16)
                    by_pair = b_qkv.rearrange("(q t j) -> t j q", t=2, j=QKV)
                    for t in range(2):
                        sp.dma_start(b_v[rows(t), :], by_pair[t, P:QKV, :],
                                 allow_slow_non_contiguous=True).then_inc(vec_loaded, 16)
            sp.wait_ge(w_lo_done, 2)
            sp.dma_start(flat[:, 0:PAIRS * C].rearrange("p (q n) -> p q n", q=PAIRS),
                         w_out.rearrange("(q p) n -> p q n", p=P)).then_inc(w_loaded, 16)
            sp.dma_start(flat[:, 2048:2560], w_guide).then_inc(w_loaded, 16)
            sp.dma_start(flat[:, 2560:3072].rearrange("p (k r) -> p k r", k=CK),
                         w_fuse.rearrange("(k p) r -> p k r", p=P)).then_inc(w_loaded, 16)

            def load_x(b, j):
                sp.wait_ge(x_lo_done, n_x(b, j - 1) if j else n_x(b - 1, 2 * CK - 1))
                sp.dma_start(x_raw[:, :], x_v[b][:, j // 2, half_cols[j % 2]]).then_inc(x_loaded, 16)

            def shift_operand(b, h, half):
                sp.wait_ge(top_row_done, n_shift(b, 2 * h + half))
                sp.dma_start(q_shift[0:DK, half, :].bitcast(F32),
                             q_both[0:DK, h % 2, half_cols[half]].bitcast(F32)).then_inc(shift_in[half], 16)
                sp.dma_start(q_shift[DK:DK + 1, half, :].bitcast(F32),
                             top_row[:, half, :].bitcast(F32)).then_inc(shift_in[half], 16)

            def spread_den(b, h, half):
                i = 2 * h + half
                sp.wait_ge(den_done, n_head_half(b, i))
                row = 0 if h % 2 == 0 else 31
                sp.dma_start(den_sp[:, :], den_rows[row:row + 1, :]).then_inc(den_spread, 16)

            def spread_rcp(b, h, half):
                i = 2 * h + half
                sp.wait_ge(rcp_done, n_head_half(b, i))
                sp.dma_start(rcp_dram[half].rearrange("(p a) -> p a", p=P), rcp_sp[:, :]).then_inc(rcp_out, 16)
                sp.wait_ge(rcp_out, n_head_half_dma(b, i))
                sp.dma_start(res[rows(h), half, :], rcp_dram[half].partition_broadcast(DK)).then_inc(rcp_in, 16)

            def attention(b, has_next):
                chunk = 0
                for h in range(HEADS):
                    for u in range(UNITS):
                        for item in beside(h, u):
                            if item[0] == "shift":
                                shift_operand(b, item[1], item[2])
                        if u == DEN_AT[0]:
                            spread_den(b, h, 0)
                        if u == DEN_AT[1] and h:
                            spread_den(b, h - 1, 1)
                        if u == RCP_AT[0]:
                            spread_rcp(b, h, 0)
                        if u == RCP_AT[1] and h:
                            spread_rcp(b, h - 1, 1)
                        if has_next and h in X_AT and u + 2 in X_AT[h]:
                            load_x(b + 1, chunk)
                            chunk += 1
                        if has_next and h == HEADS - 2 and u == UNITS - 1:
                            load_x(b + 1, chunk)
                            chunk += 1

            def end(b, has_next, items):
                spread_den(b, HEADS - 1, 1)
                spread_rcp(b, HEADS - 1, 1)
                for item in items:
                    if item[0] == "shift":
                        shift_operand(b + 1, 0, 0)
                for m in range(CK):
                    sp.wait_ge(y_done, b * CK + m + 1)
                    sp.dma_start(out_v[b][:, m, :], acc[:, m, :]).then_inc(stored, 16)
                sp.wait_ge(stored, b * (CK * 16) + CK * 16)
                if has_next:
                    sp.dma_start(acc[:, :, :], x_v[b + 1]).then_inc(acc_loaded, 16)

            for j in range(2, 2 * CK):
                load_first_x(j)
            sp.wait_ge(w_lo_done, 3)
            sp.wait_ge(tr_ps, 2)
            sp.wait_ge(b_ps, 1)
            sp.dma_start(acc[:, :, :], x_v[0]).then_inc(acc_loaded, 16)
            shift_operand(0, 0, 0)
            with sp.Fori(0, BATCH - 1) as b:
                attention(b, True)
                end(b, True, seam(True, True))
            attention(BATCH - 1, False)
            end(BATCH - 1, False, seam(True, False))

        @block.gpsimd
        def _(pool):
            nc.gpsimd.memset(ident[:, :], 0.0).then_inc(consts_done, 1)
            nc.gpsimd.memset(v_hi[:, :, :].bitcast(F32), 1.0).then_inc(consts_done, 1)
            nc.gpsimd.memset(v_lo[:, :, :].bitcast(F32), 0.0).then_inc(consts_done, 1)
            pool.wait_ge(consts_done, 3)
            nc.gpsimd.memset(k_low[DK:P, :, :].bitcast(F32), 1.0).then_inc(consts_done, 1)
            pool.wait_ge(consts_done, 4)
            nc.gpsimd.affine_select(out=ident[:, :], in_=ident[:, :], compare_op=ALU.not_equal, fill=1.0,
                                    base=0, pattern=[[-1, P]], channel_multiplier=1).then_inc(consts_done, 1)

            def split_x(b, j):
                pool.wait_ge(x_hi_done, n_x(b, j))
                cols = (slice(None), j // 2, half_cols[j % 2])
                nc.gpsimd.tensor_tensor(out=x_lo[cols], in0=x_raw[:, :], in1=x_hi[cols].bitcast(F32),
                                        op=ALU.subtract).then_inc(x_lo_done, 1)

            def split_res(b, p, half):
                pool.wait_ge(res_hi_done, n_pair_half(b, 2 * p + half))
                nc.gpsimd.tensor_tensor(out=res_lo[:, half_cols[half]], in0=res[:, half, :],
                                        in1=res_hi[:, half_cols[half]].bitcast(F32),
                                        op=ALU.subtract).then_inc(res_lo_done, 1)

            def attention(b, has_next):
                chunk = 0
                for g in range(STEPS):
                    h, u = divmod(g, UNITS)
                    if lo_done(g)[0]:
                        pool.wait_ge(p_raw_done, n_step(b, g))
                        pool.wait_ge(pv_ps, n_step(b, g - LO_BUFS))
                        nc.gpsimd.tensor_tensor(out=p_lo[:, g % LO_BUFS, :], in0=p_raw[:, g % RAW_BUFS, :],
                                                in1=p_hi[:, g % HI_BUFS, :].bitcast(F32),
                                                op=ALU.subtract).then_inc(p_lo_pool, 1)
                    if h and h % 2 == 0 and u in RES_AT:
                        split_res(b, h // 2 - 1, RES_AT.index(u))
                    if has_next and h in X_AT and u in X_AT[h]:
                        split_x(b + 1, chunk)
                        chunk += 1

            def end(b):
                split_res(b, PAIRS - 1, 0)
                split_res(b, PAIRS - 1, 1)

            for j in range(2 * CK):
                split_x(0, j)
            with pool.Fori(0, BATCH - 1) as b:
                attention(b, True)
                end(b)
            attention(BATCH - 1, False)
            end(BATCH - 1)

        @block.scalar
        def _(act):
            flat = acc[:].rearrange("p k n -> p (k n)")
            act.wait_ge(std_in, 1)
            nc.scalar.activation(tmp[:, 1, :], tmp[:, 0, :], ACT.Sqrt).then_inc(std_done, 1)

            def split_x(b, j):
                act.wait_ge(x_loaded, n_x_dma(b, j))
                nc.scalar.activation(x_hi[:, j // 2, half_cols[j % 2]], x_raw[:, :],
                                     ACT.Copy).then_inc(x_hi_done, 1)

            def qk(b, h, half):
                act.wait_ge(qk_ps, n_qk(b, 2 * h + half))
                cols = (h % 2, half_cols[half])
                nc.scalar.activation(q_both[(slice(0, DK), *cols)], ps_p[0:DK, :], ACT.Identity,
                                     bias=b_qk[0:DK, h:h + 1])
                nc.scalar.activation(k_twice[(slice(DK, P), *cols)], ps_p[DK:P, :], ACT.Identity,
                                     bias=b_qk[DK:P, h:h + 1])
                nc.scalar.activation(k_twice[(slice(0, DK), *cols)], ps_p[DK:P, :], ACT.Identity,
                                     bias=b_qk[DK:P, h:h + 1]).then_inc(qk_hi_done, 1)

            def v(b, kt):
                act.wait_ge(v_ps, n_v(b, kt))
                nc.scalar.activation(v_hi[:, kt, :].rearrange("p (h j) -> p h j", j=VW)[:, :, 0:DK],
                                     ps_s[:, kt % SCORE_BANKS, :].rearrange("p (h j) -> p h j", j=DK),
                                     ACT.Copy).then_inc(v_hi_done, 1)

            def shift(b, h, half):
                act.wait_ge(shift_ps, n_shift(b, 2 * h + half))
                if h:
                    act.wait_ge(shift_in[half], n_shift_dma(b, h - 1))
                nc.scalar.activation(top_row[:, half, :], ps_p[0:4, 0:P], ACT.Copy,
                                     scale=-1.0).then_inc(top_row_done, 1)

            def den(b, h, half):
                i = 2 * h + half
                act.wait_ge(pv_ps, n_step(b, h * UNITS + half * KT + KT - 1))
                if i:
                    act.wait_ge(den_spread, n_head_half_dma(b, i - 1))
                at = DK if h % 2 == 0 else DK - 32
                nc.scalar.activation(den_rows[:, :], ps_o[at:at + 32, half, :], ACT.Copy).then_inc(den_done, 1)

            def split_res(b, p, half):
                act.wait_ge(norm_done, n_head_half(b, 2 * (2 * p + 1) + half))
                if p:
                    act.wait_ge(out_ps, n_out(b, out_i(p - 1, half, CK - 1)))
                nc.scalar.activation(res_hi[:, half_cols[half]], res[:, half, :],
                                     ACT.Copy).then_inc(res_hi_done, 1)

            def attention(b, has_next):
                chunk = 0
                for g in range(STEPS):
                    h, u = divmod(g, UNITS)
                    act.wait_ge(score_ps, n_step(b, g))
                    if g >= HI_BUFS:
                        act.wait_ge(pv_ps, n_step(b, g - HI_BUFS))
                    nc.scalar.activation(p_hi[:, g % HI_BUFS, :], ps_s[:, g % SCORE_BANKS, :], ACT.Exp,
                                         scale=SCALE).then_inc(p_hi_done, 1)
                    if g >= RAW_BUFS:
                        by_pool, n = lo_done(g - RAW_BUFS)
                        if by_pool:
                            act.wait_ge(p_lo_pool, b * LO_POOL + n)
                        else:
                            act.wait_ge(p_lo_dve, b * LO_DVE + n)
                    nc.scalar.activation(p_raw[:, g % RAW_BUFS, :], ps_s[:, g % SCORE_BANKS, :], ACT.Exp,
                                         scale=SCALE).then_inc(p_raw_done, 1)
                    for item in beside(h, u):
                        if item[0] == "qk":
                            qk(b, item[1], item[2])
                        if item[0] == "shift":
                            shift(b, item[1], item[2])
                    if u == DEN_AT[0]:
                        den(b, h, 0)
                    if u == DEN_AT[1] and h:
                        den(b, h - 1, 1)
                    if u in RES_AT and h and h % 2 == 0:
                        split_res(b, h // 2 - 1, RES_AT.index(u))
                    if has_next and h in X_AT and u in X_AT[h]:
                        if chunk == 0:
                            act.wait_ge(qk_ps, n_qk(b, 2 * HEADS - 1))
                        split_x(b + 1, chunk)
                        chunk += 1

            def between(b, nb, items):
                for item in items:
                    if item[0] == "qk":
                        qk(nb, 0, item[1])
                    if item[0] == "v":
                        v(nb, item[1])
                    if item[0] == "shift":
                        shift(nb, 0, 0)
                    if item == ("out", 0, 0):
                        split_res(b, PAIRS - 1, 0)
                    if item == ("out", 1, 0):
                        split_res(b, PAIRS - 1, 1)

            def gate(b):
                act.wait_ge(y2_done, n_one(b, 0))
                for m in range(CK):
                    nc.scalar.activation(acc[:, m, :], acc[:, m, :], ACT.Identity,
                                         bias=y2[:, 3, m:m + 1]).then_inc(y_done, 1)

            for part in range(2):
                act.wait_ge(w_loaded, 16 * (part + 1))
                nc.scalar.activation(wqkv_hi[:, 2 * part:2 * part + 2, :].rearrange("p k n -> p (k n)"),
                                     flat[:, 0:2 * 3 * C], ACT.Copy).then_inc(w_hi_done, 1)
                split_x(0, part)
            act.wait_ge(w_loaded, 16 * 5)
            nc.scalar.activation(wout_hi[:, :, :].rearrange("p q n -> p (q n)"), flat[:, 0:PAIRS * C],
                                 ACT.Copy).then_inc(w_hi_done, 1)
            for j in range(2, 2 * CK):
                split_x(0, j)
            act.wait_ge(vec_loaded, 16 * 8)
            act.wait_ge(consts_done, 4)
            between(0, 0, seam(False, True))
            with act.Fori(0, BATCH - 1) as b:
                attention(b, True)
                den(b, HEADS - 1, 1)
                between(b, b + 1, seam(True, True))
                gate(b)
            attention(BATCH - 1, False)
            den(BATCH - 1, HEADS - 1, 1)
            between(BATCH - 1, BATCH, seam(True, False))
            gate(BATCH - 1)

        @block.vector
        def _(dve):
            flat = acc[:].rearrange("p k n -> p (k n)")
            chained = [0]

            def link(ins):
                chained[0] += 1
                ins.then_inc(set_chain, 1)
                dve.wait_ge(set_chain, chained[0])

            dve.wait_ge(vec_loaded, 16 * 8)
            nc.vector.tensor_scalar(tmp[:, 0, :], bn[:, 3, :], BN_EPS, None, ALU.add).then_inc(std_in, 1)
            dve.wait_ge(std_done, 1)
            link(nc.vector.reciprocal(tmp[:, 2, :], tmp[:, 1, :]))
            link(nc.vector.tensor_tensor(out=tmp[:, 1, :], in0=tmp[:, 2, :], in1=tmp[:, 2, :], op=ALU.mult))
            link(nc.vector.tensor_tensor(out=tmp[:, 1, :], in0=tmp[:, 1, :], in1=tmp[:, 0, :], op=ALU.mult))
            link(nc.vector.tensor_scalar(tmp[:, 1, :], tmp[:, 1, :], -0.5, 1.5, ALU.mult, ALU.add))
            link(nc.vector.tensor_tensor(out=tmp[:, 2, :], in0=tmp[:, 2, :], in1=tmp[:, 1, :], op=ALU.mult))
            link(nc.vector.tensor_tensor(out=bn_scale[:, :], in0=tmp[:, 2, :], in1=bn[:, 0, :], op=ALU.mult))
            link(nc.vector.tensor_tensor(out=tmp[:, 1, :], in0=bn_scale[:, :], in1=bn[:, 2, :], op=ALU.mult))
            link(nc.vector.tensor_tensor(out=bn_shift[:, :], in0=bn[:, 1, :], in1=tmp[:, 1, :], op=ALU.subtract))
            for part in range(2):
                dve.wait_ge(w_hi_done, part + 1)
                nc.vector.tensor_tensor(out=wqkv_lo[:, 2 * part:2 * part + 2, :].rearrange("p k n -> p (k n)"),
                                        in0=flat[:, 0:2 * 3 * C],
                                        in1=wqkv_hi[:, 2 * part:2 * part + 2, :].rearrange("p k n -> p (k n)").bitcast(F32),
                                        op=ALU.subtract).then_inc(w_lo_done, 1)
            dve.wait_ge(w_hi_done, 3)
            nc.vector.tensor_tensor(out=wout_lo[:, :, :].rearrange("p q n -> p (q n)"), in0=flat[:, 0:PAIRS * C],
                                    in1=wout_hi[:, :, :].rearrange("p q n -> p (q n)").bitcast(F32),
                                    op=ALU.subtract).then_inc(w_lo_done, 1)
            dve.wait_ge(tr_ps, 2)
            nc.vector.tensor_copy(guide_t[:, :, :].rearrange("p k r -> p (k r)"), ps_m[:, 0, :]).then_inc(tr_done, 1)
            nc.vector.tensor_copy(fuse_t[:, :], ps_m[:, 1, :]).then_inc(tr_done, 1)
            dve.wait_ge(b_ps, 1)
            nc.vector.tensor_tensor(out=b_res[:, :], in0=ps_p[:, 0:CK], in1=tmp[:, 3, :],
                                    op=ALU.add).then_inc(b_done, 1)

            def qk(b, h, half):
                dve.wait_ge(qk_hi_done, n_qk(b, 2 * h + half))
                cols = (h % 2, half_cols[half])
                nc.vector.scalar_tensor_tensor(out=q_both[(slice(DK, P), *cols)], in0=ps_p[0:DK, :],
                                               scalar=b_qk[0:DK, h:h + 1],
                                               in1=q_both[(slice(0, DK), *cols)].bitcast(F32),
                                               op0=ALU.add, op1=ALU.subtract)
                nc.vector.scalar_tensor_tensor(out=k_low[(slice(0, DK), *cols)], in0=ps_p[DK:P, :],
                                               scalar=b_qk[DK:P, h:h + 1],
                                               in1=k_twice[(slice(DK, P), *cols)].bitcast(F32),
                                               op0=ALU.add, op1=ALU.subtract).then_inc(qk_lo_done, 1)

            def v(b, kt):
                dve.wait_ge(v_hi_done, n_v(b, kt))
                cols = [t[:, kt, :].rearrange("p (h j) -> p h j", j=VW)[:, :, 0:DK] for t in (v_lo, v_hi)]
                nc.vector.tensor_tensor(out=cols[0],
                                        in0=ps_s[:, kt % SCORE_BANKS, :].rearrange("p (h j) -> p h j", j=DK),
                                        in1=cols[1].bitcast(F32), op=ALU.subtract).then_inc(v_lo_done, 1)

            def row_max(b, h, qt):
                dve.wait_ge(max_ps, n_max(b, h * KT + qt))
                nc.vector.tensor_reduce(out=top[:, h % 2, qt:qt + 1], in_=ps_m[:, :, :].rearrange("p a n -> p (a n)"),
                                        op=ALU.max, axis=AX_X).then_inc(max_done, 1)

            def out_add(b, p, half, m):
                i = out_i(p, half, m)
                dve.wait_ge(out_ps, n_out(b, i))
                if p == 0:
                    dve.wait_ge(acc_loaded, b * 16 + 16)
                else:
                    dve.wait_ge(out_done, n_out(b, i - 2 * CK))
                to = acc[:, m, half_cols[half]]
                if p < PAIRS - 1:
                    nc.vector.tensor_tensor(out=to, in0=ps_p[:, :], in1=to, op=ALU.add).then_inc(out_done, 1)
                else:
                    nc.vector.scalar_tensor_tensor(out=to, in0=ps_p[:, :], scalar=1.0, in1=to, op0=ALU.mult,
                                                   op1=ALU.add, accum_out=sums[:, m, half:half + 1]).then_inc(out_done, 1)

            def reciprocal(b, h, half):
                dve.wait_ge(den_spread, n_head_half_dma(b, 2 * h + half))
                nc.vector.reciprocal(rcp_sp[:, :], den_sp[:, :]).then_inc(rcp_done, 1)

            def normalise(b, h, half):
                dve.wait_ge(rcp_in, n_head_half_dma(b, 2 * h + half))
                nc.vector.tensor_tensor(out=res[rows(h), half, :], in0=ps_o[rows(h), half, :],
                                        in1=res[rows(h), half, :], op=ALU.mult).then_inc(norm_done, 1)

            def attention(b):
                for g in range(STEPS):
                    h, u = divmod(g, UNITS)
                    by_pool, n = lo_done(g)
                    if not by_pool:
                        dve.wait_ge(p_raw_done, n_step(b, g))
                        if g >= LO_BUFS:
                            dve.wait_ge(pv_ps, n_step(b, g - LO_BUFS))
                        nc.vector.tensor_tensor(out=p_lo[:, g % LO_BUFS, :], in0=p_raw[:, g % RAW_BUFS, :],
                                                in1=p_hi[:, g % HI_BUFS, :].bitcast(F32),
                                                op=ALU.subtract).then_inc(p_lo_dve, 1)
                    for item in beside(h, u):
                        if item[0] == "qk":
                            qk(b, item[1], item[2])
                        if item[0] == "max":
                            row_max(b, item[1], item[2])
                        if item[0] == "out":
                            out_add(b, *item[1:])
                    if u == RCP_AT[0]:
                        reciprocal(b, h, 0)
                    if u == RCP_AT[1] and h:
                        reciprocal(b, h - 1, 1)
                    if u == NORM_AT[0]:
                        normalise(b, h, 0)
                    if u == NORM_AT[1] and h:
                        normalise(b, h - 1, 1)

            gate_links = 5

            def between(b, nb, items):
                links = [0]

                def chain(ins):
                    links[0] += 1
                    ins.then_inc(gate_chain, 1)
                    dve.wait_ge(gate_chain, b * gate_links + links[0])

                for item in items:
                    if item[0] == "qk":
                        qk(nb, 0, item[1])
                    if item[0] == "v":
                        v(nb, item[1])
                    if item[0] == "max":
                        row_max(nb, 0, item[1])
                    if item == ("out", 0, 1):
                        reciprocal(b, HEADS - 1, 1)
                    if item == ("out", 1, 0):
                        normalise(b, HEADS - 1, 1)
                    if item[0] == "out":
                        out_add(b, PAIRS - 1, item[1], item[2])
                    if item == ("out", 1, CK - 1):
                        dve.wait_ge(out_done, n_out(b, out_i(PAIRS - 1, 1, CK - 1)))
                        chain(nc.vector.tensor_tensor(out=y2[:, 0, :], in0=sums[:, :, 0], in1=sums[:, :, 1], op=ALU.add))
                        nc.vector.scalar_tensor_tensor(out=avg[:, :], in0=y2[:, 0, :], scalar=1.0 / TOK, in1=b_res[:, :],
                                                       op0=ALU.mult, op1=ALU.add).then_inc(avg_done, 1)
                    if item[0] == "gate1":
                        dve.wait_ge(gate1_ps, n_one(b, 0))
                        nc.vector.tensor_scalar(y1[:, :], ps_p[:, 0:1], 0.0, 6.0, ALU.max, ALU.min).then_inc(y1_done, 1)
                    if item[0] == "gate2":
                        dve.wait_ge(gate2_ps, n_one(b, 0))
                        chain(nc.vector.tensor_tensor(out=y2[:, 1, :], in0=ps_p[:, 0:CK], in1=bn_scale[:, :], op=ALU.mult))
                        chain(nc.vector.tensor_tensor(out=y2[:, 2, :], in0=y2[:, 1, :], in1=bn_shift[:, :], op=ALU.add))
                        chain(nc.vector.tensor_scalar(y2[:, 1, :], y2[:, 2, :], 0.0, 6.0, ALU.max, ALU.min))
                        chain(nc.vector.tensor_tensor(out=y2[:, 2, :], in0=y2[:, 1, :], in1=b_res[:, :], op=ALU.add))
                        nc.vector.tensor_copy(y2[:, 3, :], y2[:, 2, :]).then_inc(y2_done, 1)

            dve.wait_ge(consts_done, 4)
            between(0, 0, seam(False, True))
            with dve.Fori(0, BATCH - 1) as b:
                attention(b)
                between(b, b + 1, seam(True, True))
            attention(BATCH - 1)
            between(BATCH - 1, BATCH, seam(True, False))

        @block.tensor
        def _(pe):
            flat = acc[:].rearrange("p k n -> p (k n)")
            mm = nc.tensor.matmul

            pe.wait_ge(consts_done, 5)
            pe.wait_ge(w_loaded, 16 * 5)
            pe.wait_ge(vec_loaded, 16 * 8)
            for k in range(CK):
                done = nc.tensor.transpose(ps_m[:, 0, k * P:(k + 1) * P], flat[:, 2048 + k * P:2048 + (k + 1) * P], ident[:, :])
            done.then_inc(tr_ps, 1)
            for k in range(CK):
                done = nc.tensor.transpose(ps_m[:, 1, k * P:(k + 1) * P], flat[:, 2560 + k * P:2560 + (k + 1) * P], ident[:, :])
            done.then_inc(tr_ps, 1)
            for m in range(CK):
                for q in range(PAIRS):
                    done = mm(ps_p[:, m:m + 1], flat[:, q * C + m * P:q * C + (m + 1) * P], b_v[:, q:q + 1],
                              start=(q == 0), stop=(q == PAIRS - 1))
            done.then_inc(b_ps, 1)

            def split3(to, pairs):
                n = 3 * len(pairs)
                i = 0
                for a_hi, a_lo, b_hi, b_lo in pairs:
                    for a, c in ((a_hi, b_hi), (a_hi, b_lo), (a_lo, b_hi)):
                        done = mm(to, a, c, start=(i == 0), stop=(i == n - 1))
                        i += 1
                return done

            def qk(b, h, half, free):
                free()
                if h == 0:
                    pe.wait_ge(x_lo_done, n_x(b, 2 * CK - 1))
                w, t = slice(h * QKV, h * QKV + P), half_cols[half]
                split3(ps_p[:, :], [(wqkv_hi[:, k, w], wqkv_lo[:, k, w], x_hi[:, k, t], x_lo[:, k, t])
                                    for k in range(CK)]).then_inc(qk_ps, 1)

            def v(b, kt):
                if kt >= SCORE_BANKS:
                    pe.wait_ge(v_lo_done, n_v(b, kt - SCORE_BANKS))
                t = slice(kt * P, (kt + 1) * P)
                w_v = [w[:, :, :].rearrange("p k (h j) -> p k h j", j=QKV)[:, :, :, P:QKV] for w in (wqkv_hi, wqkv_lo)]
                split3(ps_s[:, kt % SCORE_BANKS, :], [(x_hi[:, k, t], x_lo[:, k, t], w_v[0][:, k], w_v[1][:, k])
                                                      for k in range(CK)]).then_inc(v_ps, 1)

            def row_max(b, h, qt):
                if qt == 0:
                    pe.wait_ge(qk_lo_done, n_qk(b, 2 * h + 1))
                if qt or h:
                    pe.wait_ge(max_done, n_max(b, h * KT + qt - 1))
                for kh in range(2):
                    done = mm(ps_m[:, kh, :], q_both[:, h % 2, qt * P:(qt + 1) * P],
                              k_twice[:, h % 2, half_cols[kh]], start=True, stop=True)
                done.then_inc(max_ps, 1)

            def shift(b, h, half, free):
                free()
                pe.wait_ge(max_done, n_max(b, h * KT + 4 * half + 3))
                nc.tensor.transpose(ps_p[0:4, 0:P], top[:, h % 2, 4 * half:4 * half + 4],
                                    ident[:, :]).then_inc(shift_ps, 1)

            def out_proj(b, p, half, m, free):
                free()
                pe.wait_ge(res_lo_done, n_pair_half(b, 2 * p + half))
                w, t = slice(m * P, (m + 1) * P), half_cols[half]
                split3(ps_p[:, :], [(wout_hi[:, p, w], wout_lo[:, p, w], res_hi[:, t], res_lo[:, t])]).then_inc(out_ps, 1)

            def scores(b, g):
                h, u = divmod(g, UNITS)
                half, kt = divmod(u, KT)
                if g >= SCORE_BANKS:
                    pe.wait_ge(p_raw_done, n_step(b, g - SCORE_BANKS))
                else:
                    pe.wait_ge(v_lo_done, n_v(b, KT - 1))
                if kt == 0:
                    pe.wait_ge(shift_in[half], n_shift_dma(b, h))
                keys = slice(kt * P, (kt + 1) * P)
                to = ps_s[:, g % SCORE_BANKS, :]
                mm(to, k_twice[:, h % 2, keys], q_both[:, h % 2, half_cols[half]], start=True, stop=False)
                mm(to, k_low[0:DK + 1, h % 2, keys], q_shift[0:DK + 1, half, :],
                   start=False, stop=True).then_inc(score_ps, 1)

            def values(b, g):
                h, u = divmod(g, UNITS)
                half, kt = divmod(u, KT)
                if kt == 0 and h:
                    pe.wait_ge(norm_done, n_head_half(b, 2 * (h - 1) + half))
                at = h * VW if h % 2 == 0 else h * VW - DK
                cols = slice(at, at + P)
                to = ps_o[:, half, :]
                pe.wait_ge(p_hi_done, n_step(b, g))
                mm(to, v_hi[:, kt, cols], p_hi[:, g % HI_BUFS, :], start=(kt == 0), stop=False)
                mm(to, v_lo[:, kt, cols], p_hi[:, g % HI_BUFS, :], start=False, stop=False)
                by_pool, n = lo_done(g)
                if by_pool:
                    pe.wait_ge(p_lo_pool, b * LO_POOL + n)
                else:
                    pe.wait_ge(p_lo_dve, b * LO_DVE + n)
                mm(to, v_hi[:, kt, cols], p_lo[:, g % LO_BUFS, :], start=False, stop=(kt == KT - 1)).then_inc(pv_ps, 1)

            reader = [None]

            def free():
                if reader[0]:
                    pe.wait_ge(*reader[0])

            def shared(item, b):
                kind = item[0]
                if kind == "qk":
                    qk(b, item[1], item[2], free)
                    reader[0] = (qk_lo_done, n_qk(b, 2 * item[1] + item[2]))
                if kind == "shift":
                    shift(b, item[1], item[2], free)
                    reader[0] = (top_row_done, n_shift(b, 2 * item[1] + item[2]))
                if kind == "out":
                    out_proj(b, *item[1:], free)
                    reader[0] = (out_done, n_out(b, out_i(*item[1:])))

            def attention(b):
                reader[0] = (top_row_done, n_shift(b, 0))
                for g in range(STEPS + LAG):
                    if g < STEPS:
                        scores(b, g)
                    if g >= LAG:
                        values(b, g - LAG)
                    if g < STEPS:
                        for item in beside(*divmod(g, UNITS)):
                            if item[0] == "max":
                                row_max(b, item[1], item[2])
                            else:
                                shared(item, b)

            def between(b, nb, items):
                for item in items:
                    if item[0] == "qk":
                        shared(("qk", 0, item[1]), nb)
                    if item[0] == "v":
                        v(nb, item[1])
                    if item[0] == "max":
                        row_max(nb, 0, item[1])
                    if item[0] == "shift":
                        shared(("shift", 0, 0), nb)
                    if item[0] == "out":
                        shared(("out", PAIRS - 1, item[1], item[2]), b)
                    if item[0] == "gate1":
                        free()
                        pe.wait_ge(avg_done, n_one(b, 0))
                        for k in range(CK):
                            done = mm(ps_p[:, 0:1], guide_t[:, k, :], avg[:, k:k + 1], start=(k == 0), stop=(k == CK - 1))
                        done.then_inc(gate1_ps, 1)
                        reader[0] = (y1_done, n_one(b, 0))
                    if item[0] == "gate2":
                        free()
                        for m in range(CK):
                            done = mm(ps_p[:, m:m + 1], fuse_t[:, m * P:(m + 1) * P], y1[:, :], start=True, stop=True)
                        done.then_inc(gate2_ps, 1)
                        reader[0] = (y2_done, n_one(b, 0))

            pe.wait_ge(w_lo_done, 3)
            pe.wait_ge(tr_done, 2)
            reader[0] = (b_done, 1)
            between(0, 0, seam(False, True))
            with pe.Fori(0, BATCH - 1) as b:
                attention(b)
                between(b, b + 1, seam(True, True))
            attention(BATCH - 1)
            between(BATCH - 1, BATCH, seam(True, False))


_INS = ["x", "L0_conv_W_qkv", "L0_conv_b_qkv", "L0_conv_W_out", "L0_conv_b_out", "L1_conv_w_guide", "L1_conv_w_fuse",
        "L1_conv_bn_gamma", "L1_conv_bn_beta", "L1_conv_bn_mean", "L1_conv_bn_var"]
_OUTS = [((16, 512, 32, 32), "float32")]


def kernel(**inputs):
    import numpy as _np
    import concourse.bacc as _bacc
    from concourse import mybir as _mybir
    from concourse.bass_utils import run_bass_kernel_spmd as _run

    nc = _bacc.Bacc("TRN2", target_bir_lowering=False, num_devices=1, dynamic_dma_scratch_size=4096)
    arrays, args = {}, []
    for name in _INS:
        a = _np.ascontiguousarray(inputs[name])
        arrays[f"in_{name}_dram"] = a
        args.append(nc.dram_tensor(f"in_{name}_dram", a.shape, _mybir.dt.from_np(a.dtype), kind="ExternalInput").ap())
    for i, (shape, dtype) in enumerate(_OUTS):
        dt = _mybir.dt.from_np(_np.dtype(dtype))
        args.append(nc.dram_tensor(f"out_{i}_dram", shape, dt, kind="ExternalOutput").ap())
    attention_block_kernel(nc, *args)
    r = _run(nc, [arrays], core_ids=[0])
    return r.results[0]["out_0_dram"]
```

```python
from contextlib import ExitStack

import concourse.bass as bass
from concourse import mybir

P = 128
F32 = mybir.dt.float32
F32R = mybir.dt.float32r
ALU = mybir.AluOpType
ACT = mybir.ActivationFunctionType
AX_X = mybir.AxisListType.X

BATCH, C, TOK = 16, 512, 1024
HEADS, DK, RED = 8, 64, 128
CK = C // P
HALF = TOK // 2
KT = TOK // P
PAIRS = HEADS // 2
UNITS = 2 * KT
STEPS = HEADS * UNITS
QKV = 3 * DK
VW = DK + 1
LAG = 3
SCORE_BANKS, HI_BUFS, LO_BUFS, RAW_BUFS = 3, 4, 3, 3
SCALE = DK ** -0.5
BN_EPS = 1e-5

QK_AT = {0: 0, 3: 1}
MAX_ORDER = [(4 * half + qt, kh) for half in range(2) for kh in range(2) for qt in range(4)]
MAX_FROM = 3
MAX_LATE = MAX_FROM + len(MAX_ORDER) - UNITS
SHIFT1_AT, SHIFT0_AT = 5, 12
COPY1_AT, COPY0_AT = 1, 9
OUT_AT = {7: 0, 9: 1, 11: 2, 14: 3}
POOL_LO = (4, 7, 10, 13)
DEN_AT, RCP_AT, NORM_AT, RES_AT = (11, 3), (13, 5), (0, 8), (1, 9)
X_AHEAD = 4
X_AT = {6: (5, 8, 11, 14), 7: (1, 4, 7, 10)}

TAIL_OUT_AT = {6: (0, 0), 7: (0, 1), 8: (0, 2), 9: (0, 3), 10: (1, 0), 11: (1, 1), 13: (1, 2), 14: (1, 3)}
GATE_AT = {(1, 6): ("gate1",), (1, 7): ("gate2",)}
ADD_GATE_AT, STORE_AT, ACC_AT = (8, 9, 10, 11), (9, 10, 11, 12), (12, 13, 14, 15)
HEAD2 = 2 * UNITS

SEAM = [("qk", 0), ("pv", STEPS - 3), ("v", 0), ("pv", STEPS - 2), ("pv", STEPS - 1), ("v", 1), ("qk", 1), ("max", 0),
        ("max", 1), ("v", 2), ("max", 2), ("max", 3), ("v", 3), ("max", 4), ("max", 5), ("v", 4), ("max", 6),
        ("max", 7), ("v", 5), ("max", 8), ("shift",), ("max", 9), ("v", 6), ("max", 10), ("v", 7), ("max", 11),
        ("max", 12)]


def beside(h, u):
    items = []
    if u in QK_AT and h + 1 < HEADS:
        items.append(("qk", h + 1, QK_AT[u]))
    if u == SHIFT1_AT:
        items.append(("shift", h, 1))
    if u in OUT_AT and h > 1:
        items.append(("out", h // 2 - 1, h % 2, OUT_AT[u]))
    if u < MAX_LATE:
        items.append(("max", h, u + UNITS - MAX_FROM))
    if u >= MAX_FROM and h + 1 < HEADS:
        items.append(("max", h + 1, u - MAX_FROM))
    if u == SHIFT0_AT and h + 1 < HEADS:
        items.append(("shift", h + 1, 0))
    return items


def tail(h, u):
    items = []
    if h == 0 and u in TAIL_OUT_AT:
        items.append(("out", PAIRS - 1, *TAIL_OUT_AT[u]))
    if (h, u) in GATE_AT:
        items.append(GATE_AT[h, u])
    return items


TAIL = [i for h in range(2) for u in range(UNITS) for i in tail(h, u)]


def lo_done(g):
    pool = g % UNITS in POOL_LO
    return pool, sum((i % UNITS in POOL_LO) == pool for i in range(g + 1))


LO_POOL = HEADS * len(POOL_LO)
LO_DVE = STEPS - LO_POOL


def attention_block_kernel(nc, x, w_qkv, b_qkv, w_out, b_out, w_guide, w_fuse, gamma, beta, mean, var, out):
    x_v = x.rearrange("b (k p) h w -> b p k (h w)", p=P)
    out_v = out.rearrange("b (k p) h w -> b p k (h w)", p=P)
    wq_v = w_qkv.rearrange("(k p) n -> p k n", p=P)

    with ExitStack() as ctx:
        def sb(name, shape, dt=F32):
            return ctx.enter_context(nc.sbuf_tensor(name, shape, dt))

        def sem(name):
            return ctx.enter_context(nc.semaphore(name))

        wqkv_hi = sb("wqkv_hi", [P, CK, 3 * C], F32R)
        wqkv_lo = sb("wqkv_lo", [P, CK, 3 * C], F32R)
        wout_hi = sb("wout_hi", [P, PAIRS, C], F32R)
        wout_lo = sb("wout_lo", [P, PAIRS, C], F32R)
        x_hi = sb("x_hi", [P, CK, TOK], F32R)
        x_lo = sb("x_lo", [P, CK, TOK], F32R)
        x_raw = sb("x_raw", [P, 2, HALF])
        v_hi = sb("v_hi", [P, KT, HEADS * VW], F32R)
        v_lo = sb("v_lo", [P, KT, HEADS * VW], F32R)
        q_both = sb("q_both", [P, 2, TOK], F32R)
        k_twice = sb("k_twice", [P, 2, TOK], F32R)
        k_low = sb("k_low", [P, 2, TOK], F32R)
        q_shift = sb("q_shift", [P, 2, HALF], F32R)
        p_raw = sb("p_raw", [P, RAW_BUFS, HALF])
        p_hi = sb("p_hi", [P, HI_BUFS, HALF], F32R)
        p_lo = sb("p_lo", [P, LO_BUFS, HALF], F32R)
        acc = sb("acc", [P, CK, TOK])
        res_hi = sb("res_hi", [P, TOK], F32R)
        res_lo = sb("res_lo", [P, TOK], F32R)
        den_rows = sb("den_rows", [32, HALF])
        res = sb("res", [P, 2, HALF])
        den_sp = sb("den_sp", [P, HALF // P])
        rcp_sp = sb("rcp_sp", [P, HALF // P])
        top_half = sb("top_half", [P, 2, KT, 2])
        top = sb("top", [P, 2, KT])
        top_row = sb("top_row", [4, 2, P], F32R)
        ident = sb("ident", [P, P])
        guide_t = sb("guide_t", [P, CK, RED])
        fuse_t = sb("fuse_t", [P, C])
        b_qk = sb("b_qk", [P, HEADS])
        b_v = sb("b_v", [P, PAIRS])
        b_res = sb("b_res", [P, CK])
        bn = sb("bn", [P, 4, CK])
        bn_scale = sb("bn_scale", [P, CK])
        bn_shift = sb("bn_shift", [P, CK])
        tmp = sb("tmp", [P, 4, CK])
        sums = sb("sums", [P, CK, 2])
        avg = sb("avg", [P, CK])
        y1 = sb("y1", [P, 1])
        y2 = sb("y2", [P, 4, CK])
        rcp_dram = nc.dram_tensor("rcp_dram", [2, HALF], F32, kind="Internal").ap()

        ps_s = ctx.enter_context(nc.psum_tensor("ps_s", [P, SCORE_BANKS, HALF], F32))
        ps_o = ctx.enter_context(nc.psum_tensor("ps_o", [P, 2, HALF], F32))
        ps_m = ctx.enter_context(nc.psum_tensor("ps_m", [P, 2, HALF], F32))
        ps_p = ctx.enter_context(nc.psum_tensor("ps_p", [P, HALF], F32))

        w_loaded = sem("w_loaded")
        w_hi_done = sem("w_hi_done")
        w_lo_done = sem("w_lo_done")
        vec_loaded = sem("vec_loaded")
        consts_done = sem("consts_done")
        tr_ps = sem("tr_ps")
        tr_done = sem("tr_done")
        b_ps = sem("b_ps")
        b_done = sem("b_done")
        std_in = sem("std_in")
        std_done = sem("std_done")
        set_chain = sem("set_chain")
        x_loaded = [sem("x_loaded0"), sem("x_loaded1")]
        x_hi_done = sem("x_hi_done")
        x_lo_done = sem("x_lo_done")
        acc_loaded = [sem(f"acc_loaded{m}") for m in range(CK)]
        qk_ps = sem("qk_ps")
        v_ps = sem("v_ps")
        max_ps = sem("max_ps")
        shift_ps = sem("shift_ps")
        score_ps = sem("score_ps")
        pv_ps = sem("pv_ps")
        out_ps = sem("out_ps")
        gate1_ps = sem("gate1_ps")
        gate2_ps = sem("gate2_ps")
        qk_hi_done = sem("qk_hi_done")
        v_hi_done = sem("v_hi_done")
        top_row_done = sem("top_row_done")
        p_hi_done = sem("p_hi_done")
        p_raw_done = sem("p_raw_done")
        den_done = sem("den_done")
        res_hi_done = sem("res_hi_done")
        y_done = sem("y_done")
        qk_lo_done = sem("qk_lo_done")
        v_lo_done = sem("v_lo_done")
        max_done = sem("max_done")
        top_done = sem("top_done")
        p_lo_dve = sem("p_lo_dve")
        rcp_done = sem("rcp_done")
        norm_done = sem("norm_done")
        out_done = sem("out_done")
        avg_done = sem("avg_done")
        y1_done = sem("y1_done")
        y2_done = sem("y2_done")
        gate_chain = sem("gate_chain")
        p_lo_pool = sem("p_lo_pool")
        res_lo_done = sem("res_lo_done")
        k_in = [sem("k_in0"), sem("k_in1")]
        shift_in = [sem("shift_in0"), sem("shift_in1")]
        den_spread = sem("den_spread")
        rcp_out = sem("rcp_out")
        rcp_in = sem("rcp_in")
        stored = [sem(f"stored{m}") for m in range(CK)]

        half_cols = [slice(0, HALF), slice(HALF, TOK)]

        def rows(h):
            return slice(DK * (h % 2), DK * (h % 2) + DK)

        def last(n, m=1):
            return lambda b, i: b * (n * m) + (i + 1) * m

        n_qk = n_shift = n_head_half = last(2 * HEADS)
        n_pair_half = last(2 * PAIRS)
        n_v = last(KT)
        n_max = last(HEADS * 2 * KT)
        n_top = last(2 * HEADS)
        n_step = last(STEPS)
        n_out = last(PAIRS * 2 * CK)
        n_one = last(1)
        n_x = last(2 * CK)
        n_x_dma = last(CK, 16)
        n_shift_dma = last(HEADS, 32)
        n_head_dma = last(HEADS, 16)
        n_head_half_dma = last(2 * HEADS, 16)
        out_i = lambda p, half, m: (p * 2 + half) * CK + m

        block = ctx.enter_context(nc.Block())

        @block.sync
        def _(sp):
            flat = acc[:].rearrange("p k n -> p (k n)")
            def load_first_x(j):
                if j > 1:
                    sp.wait_ge(x_lo_done, j - 1)
                sp.dma_start(x_raw[:, j % 2, :], x_v[0][:, j // 2, half_cols[j % 2]]).then_inc(x_loaded[j % 2], 16)

            for part in range(2):
                if part:
                    sp.wait_ge(w_lo_done, 1)
                sp.dma_start(flat[:, 0:2 * 3 * C].rearrange("p (k n) -> p k n", k=2),
                             wq_v[:, 2 * part:2 * part + 2, :]).then_inc(w_loaded, 16)
                load_first_x(part)
                if part == 0:
                    sp.dma_start(bn[:, 0, :], gamma.rearrange("(k p) -> p k", p=P),
                                 allow_slow_non_contiguous=True).then_inc(vec_loaded, 16)
                    sp.dma_start(bn[:, 1, :], beta.rearrange("(k p) -> p k", p=P),
                                 allow_slow_non_contiguous=True).then_inc(vec_loaded, 16)
                    sp.dma_start(bn[:, 2, :], mean.rearrange("(k p) -> p k", p=P),
                                 allow_slow_non_contiguous=True).then_inc(vec_loaded, 16)
                    sp.dma_start(bn[:, 3, :], var.rearrange("(k p) -> p k", p=P),
                                 allow_slow_non_contiguous=True).then_inc(vec_loaded, 16)
                    sp.dma_start(tmp[:, 3, :], b_out.rearrange("(k p) -> p k", p=P),
                                 allow_slow_non_contiguous=True).then_inc(vec_loaded, 16)
                    sp.dma_start(b_qk[:, :], b_qkv.rearrange("(h j) -> j h", j=QKV)[0:P, :],
                                 allow_slow_non_contiguous=True).then_inc(vec_loaded, 16)
                    by_pair = b_qkv.rearrange("(q t j) -> t j q", t=2, j=QKV)
                    for t in range(2):
                        sp.dma_start(b_v[rows(t), :], by_pair[t, P:QKV, :],
                                 allow_slow_non_contiguous=True).then_inc(vec_loaded, 16)
            sp.wait_ge(w_lo_done, 2)
            sp.dma_start(flat[:, 0:PAIRS * C].rearrange("p (q n) -> p q n", q=PAIRS),
                         w_out.rearrange("(q p) n -> p q n", p=P)).then_inc(w_loaded, 16)
            sp.dma_start(flat[:, 2048:2560], w_guide).then_inc(w_loaded, 16)
            sp.dma_start(flat[:, 2560:3072].rearrange("p (k r) -> p k r", k=CK),
                         w_fuse.rearrange("(k p) r -> p k r", p=P)).then_inc(w_loaded, 16)

            def load_x(b, j):
                sp.wait_ge(x_lo_done, n_x(b, j - 2) if j > 1 else n_x(b - 1, 2 * CK - 2 + j))
                sp.dma_start(x_raw[:, j % 2, :], x_v[b][:, j // 2, half_cols[j % 2]]).then_inc(x_loaded[j % 2], 16)

            def twice(b, h, half):
                sp.wait_ge(qk_hi_done, n_qk(b, 2 * h + half))
                cols = (h % 2, half_cols[half])
                sp.dma_start(k_twice[(slice(0, DK), *cols)].bitcast(F32),
                             k_twice[(slice(DK, P), *cols)].bitcast(F32)).then_inc(k_in[half], 16)

            def copy_q(b, h, half):
                if h:
                    sp.wait_ge(score_ps, n_step(b, (h - 1) * UNITS + half * KT + KT - 1))
                sp.dma_start(q_shift[0:DK, half, :].bitcast(F32),
                             q_both[0:DK, h % 2, half_cols[half]].bitcast(F32)).then_inc(shift_in[half], 16)

            def shift_operand(b, h, half):
                sp.wait_ge(top_row_done, n_shift(b, 2 * h + half))
                sp.dma_start(q_shift[DK:DK + 1, half, :].bitcast(F32),
                             top_row[:, half, :].bitcast(F32)).then_inc(shift_in[half], 16)

            def spread_den(b, h, half):
                i = 2 * h + half
                sp.wait_ge(den_done, n_head_half(b, i))
                row = 0 if h % 2 == 0 else 31
                sp.dma_start(den_sp[:, :], den_rows[row:row + 1, :]).then_inc(den_spread, 16)

            def spread_rcp(b, h, half):
                i = 2 * h + half
                sp.wait_ge(rcp_done, n_head_half(b, i))
                sp.dma_start(rcp_dram[half].rearrange("(p a) -> p a", p=P), rcp_sp[:, :]).then_inc(rcp_out, 16)
                sp.wait_ge(rcp_out, n_head_half_dma(b, i))
                sp.dma_start(res[rows(h), half, :], rcp_dram[half].partition_broadcast(DK)).then_inc(rcp_in, 16)

            def store(b, m):
                sp.wait_ge(y_done, b * CK + m + 1)
                sp.dma_start(out_v[b][:, m, :], acc[:, m, :]).then_inc(stored[m], 16)

            def load_acc(b, m):
                sp.dma_start(acc[:, m, :], x_v[b][:, m, :]).then_inc(acc_loaded[m], 16)

            def attention(b, first, end, prev, has_next):
                chunk = 0
                for g in range(first, end):
                    h, u = divmod(g, UNITS)
                    if u == COPY1_AT:
                        copy_q(b, h, 1)
                    if u == COPY0_AT and h + 1 < HEADS:
                        copy_q(b, h + 1, 0)
                    for item in beside(h, u):
                        if item[0] == "shift":
                            shift_operand(b, item[1], item[2])
                        if item[0] == "qk":
                            twice(b, item[1], item[2])
                    if u == DEN_AT[0]:
                        spread_den(b, h, 0)
                    if u == DEN_AT[1] and h:
                        spread_den(b, h - 1, 1)
                    if u == RCP_AT[0]:
                        spread_rcp(b, h, 0)
                    if u == RCP_AT[1] and h:
                        spread_rcp(b, h - 1, 1)
                    if prev and h == 1 and u in STORE_AT:
                        store(b - 1, STORE_AT.index(u))
                    if prev and h == 1 and u in ACC_AT:
                        m = ACC_AT.index(u)
                        sp.wait_ge(stored[m], b * 16)
                        load_acc(b, m)
                    h_x, u_x = divmod(g + X_AHEAD, UNITS)
                    if has_next and u_x in X_AT.get(h_x, ()):
                        load_x(b + 1, chunk)
                        chunk += 1

            def seam(b):
                for item in SEAM:
                    if item[0] == "qk":
                        twice(b + 1, 0, item[1])
                        if item[1] == 0:
                            copy_q(b + 1, 0, 0)
                    if item == ("pv", STEPS - 1):
                        spread_den(b, HEADS - 1, 1)
                    if item == ("v", 2):
                        spread_rcp(b, HEADS - 1, 1)
                    if item[0] == "shift":
                        shift_operand(b + 1, 0, 0)

            for j in range(2, 2 * CK):
                load_first_x(j)
            sp.wait_ge(w_lo_done, 3)
            sp.wait_ge(tr_ps, 2)
            sp.wait_ge(b_ps, 1)
            for m in range(CK):
                load_acc(0, m)
            for half in range(2):
                twice(0, 0, half)
            copy_q(0, 0, 0)
            shift_operand(0, 0, 0)
            attention(0, 0, HEAD2, False, True)
            with sp.Fori(0, BATCH - 1) as b:
                attention(b, HEAD2, STEPS, True, True)
                seam(b)
                attention(b + 1, 0, HEAD2, True, True)
            attention(BATCH - 1, HEAD2, STEPS, True, False)
            spread_den(BATCH - 1, HEADS - 1, 1)
            spread_rcp(BATCH - 1, HEADS - 1, 1)
            for m in range(CK):
                store(BATCH - 1, m)
            for m in range(CK):
                sp.wait_ge(stored[m], BATCH * 16)

        @block.gpsimd
        def _(pool):
            nc.gpsimd.memset(ident[:, :], 0.0).then_inc(consts_done, 1)
            nc.gpsimd.memset(v_hi[:, :, :].bitcast(F32), 1.0).then_inc(consts_done, 1)
            nc.gpsimd.memset(v_lo[:, :, :].bitcast(F32), 0.0).then_inc(consts_done, 1)
            pool.wait_ge(consts_done, 3)
            nc.gpsimd.memset(k_low[DK:P, :, :].bitcast(F32), 1.0).then_inc(consts_done, 1)
            pool.wait_ge(consts_done, 4)
            nc.gpsimd.affine_select(out=ident[:, :], in_=ident[:, :], compare_op=ALU.not_equal, fill=1.0,
                                    base=0, pattern=[[-1, P]], channel_multiplier=1).then_inc(consts_done, 1)

            def split_x(b, j):
                pool.wait_ge(x_hi_done, n_x(b, j))
                cols = (slice(None), j // 2, half_cols[j % 2])
                nc.gpsimd.tensor_tensor(out=x_lo[cols], in0=x_raw[:, j % 2, :], in1=x_hi[cols].bitcast(F32),
                                        op=ALU.subtract).then_inc(x_lo_done, 1)

            def split_res(b, p, half):
                pool.wait_ge(res_hi_done, n_pair_half(b, 2 * p + half))
                nc.gpsimd.tensor_tensor(out=res_lo[:, half_cols[half]], in0=res[:, half, :],
                                        in1=res_hi[:, half_cols[half]].bitcast(F32),
                                        op=ALU.subtract).then_inc(res_lo_done, 1)

            def attention(b, first, end, has_next):
                chunk = 0
                for g in range(first, end):
                    h, u = divmod(g, UNITS)
                    if lo_done(g)[0]:
                        pool.wait_ge(p_raw_done, n_step(b, g))
                        if g >= LO_BUFS:
                            pool.wait_ge(pv_ps, n_step(b, g - LO_BUFS))
                        nc.gpsimd.tensor_tensor(out=p_lo[:, g % LO_BUFS, :], in0=p_raw[:, g % RAW_BUFS, :],
                                                in1=p_hi[:, g % HI_BUFS, :].bitcast(F32),
                                                op=ALU.subtract).then_inc(p_lo_pool, 1)
                    if h and h % 2 == 0 and u in RES_AT:
                        split_res(b, h // 2 - 1, RES_AT.index(u))
                    if has_next and h in X_AT and u in X_AT[h]:
                        split_x(b + 1, chunk)
                        chunk += 1

            def end(b):
                split_res(b, PAIRS - 1, 0)
                split_res(b, PAIRS - 1, 1)

            for j in range(2 * CK):
                split_x(0, j)
            attention(0, 0, HEAD2, True)
            with pool.Fori(0, BATCH - 1) as b:
                attention(b, HEAD2, STEPS, True)
                end(b)
                attention(b + 1, 0, HEAD2, True)
            attention(BATCH - 1, HEAD2, STEPS, False)
            end(BATCH - 1)

        @block.scalar
        def _(act):
            flat = acc[:].rearrange("p k n -> p (k n)")
            act.wait_ge(std_in, 1)
            nc.scalar.activation(tmp[:, 1, :], tmp[:, 0, :], ACT.Sqrt).then_inc(std_done, 1)

            def split_x(b, j):
                act.wait_ge(x_loaded[j % 2], n_x_dma(b, j // 2))
                nc.scalar.activation(x_hi[:, j // 2, half_cols[j % 2]], x_raw[:, j % 2, :],
                                     ACT.Copy).then_inc(x_hi_done, 1)

            def qk(b, h, half):
                act.wait_ge(qk_ps, n_qk(b, 2 * h + half))
                cols = (h % 2, half_cols[half])
                nc.scalar.activation(q_both[(slice(0, DK), *cols)], ps_p[0:DK, :], ACT.Identity,
                                     bias=b_qk[0:DK, h:h + 1])
                nc.scalar.activation(k_twice[(slice(DK, P), *cols)], ps_p[DK:P, :], ACT.Identity,
                                     bias=b_qk[DK:P, h:h + 1]).then_inc(qk_hi_done, 1)

            def v(b, kt):
                act.wait_ge(v_ps, n_v(b, kt))
                nc.scalar.activation(v_hi[:, kt, :].rearrange("p (h j) -> p h j", j=VW)[:, :, 0:DK],
                                     ps_s[:, kt % SCORE_BANKS, :].rearrange("p (h j) -> p h j", j=DK),
                                     ACT.Copy).then_inc(v_hi_done, 1)

            def shift(b, h, half):
                act.wait_ge(shift_ps, n_shift(b, 2 * h + half))
                if h:
                    act.wait_ge(shift_in[half], n_shift_dma(b, h - 1))
                nc.scalar.activation(top_row[:, half, :], ps_p[0:4, 0:P], ACT.Copy,
                                     scale=-1.0).then_inc(top_row_done, 1)

            def den(b, h, half):
                i = 2 * h + half
                act.wait_ge(pv_ps, n_step(b, h * UNITS + half * KT + KT - 1))
                if i:
                    act.wait_ge(den_spread, n_head_half_dma(b, i - 1))
                at = DK if h % 2 == 0 else DK - 32
                nc.scalar.activation(den_rows[:, :], ps_o[at:at + 32, half, :], ACT.Copy).then_inc(den_done, 1)

            def split_res(b, p, half):
                act.wait_ge(norm_done, n_head_half(b, 2 * (2 * p + 1) + half))
                if p:
                    act.wait_ge(out_ps, n_out(b, out_i(p - 1, half, CK - 1)))
                nc.scalar.activation(res_hi[:, half_cols[half]], res[:, half, :],
                                     ACT.Copy).then_inc(res_hi_done, 1)

            def attention(b, first, end, prev, has_next):
                chunk = 0
                for g in range(first, end):
                    h, u = divmod(g, UNITS)
                    act.wait_ge(score_ps, n_step(b, g))
                    if g >= HI_BUFS:
                        act.wait_ge(pv_ps, n_step(b, g - HI_BUFS))
                    nc.scalar.activation(p_hi[:, g % HI_BUFS, :], ps_s[:, g % SCORE_BANKS, :], ACT.Exp,
                                         scale=SCALE).then_inc(p_hi_done, 1)
                    if g >= RAW_BUFS:
                        by_pool, n = lo_done(g - RAW_BUFS)
                        if by_pool:
                            act.wait_ge(p_lo_pool, b * LO_POOL + n)
                        else:
                            act.wait_ge(p_lo_dve, b * LO_DVE + n)
                    nc.scalar.activation(p_raw[:, g % RAW_BUFS, :], ps_s[:, g % SCORE_BANKS, :], ACT.Exp,
                                         scale=SCALE).then_inc(p_raw_done, 1)
                    for item in beside(h, u):
                        if item[0] == "qk":
                            qk(b, item[1], item[2])
                        if item[0] == "shift":
                            shift(b, item[1], item[2])
                    if u == DEN_AT[0]:
                        den(b, h, 0)
                    if u == DEN_AT[1] and h:
                        den(b, h - 1, 1)
                    if u in RES_AT and h and h % 2 == 0:
                        split_res(b, h // 2 - 1, RES_AT.index(u))
                    if has_next and h in X_AT and u in X_AT[h]:
                        if chunk == 0:
                            act.wait_ge(qk_ps, n_qk(b, 2 * HEADS - 1))
                        split_x(b + 1, chunk)
                        chunk += 1
                    if prev and h == 1 and u in ADD_GATE_AT:
                        add_gate(b - 1, ADD_GATE_AT.index(u))

            def seam(b, nb, prev):
                for item in SEAM:
                    if item[0] == "qk":
                        qk(nb, 0, item[1])
                    if item[0] == "v":
                        v(nb, item[1])
                    if item[0] == "shift":
                        shift(nb, 0, 0)
                    if prev and item == ("pv", STEPS - 1):
                        den(b, HEADS - 1, 1)
                    if prev and item == ("v", 1):
                        split_res(b, PAIRS - 1, 0)
                    if prev and item == ("v", 5):
                        split_res(b, PAIRS - 1, 1)

            def add_gate(b, m):
                act.wait_ge(y2_done, n_one(b, 0))
                nc.scalar.activation(acc[:, m, :], acc[:, m, :], ACT.Identity,
                                     bias=y2[:, 3, m:m + 1]).then_inc(y_done, 1)

            for part in range(2):
                act.wait_ge(w_loaded, 16 * (part + 1))
                nc.scalar.activation(wqkv_hi[:, 2 * part:2 * part + 2, :].rearrange("p k n -> p (k n)"),
                                     flat[:, 0:2 * 3 * C], ACT.Copy).then_inc(w_hi_done, 1)
                split_x(0, part)
            act.wait_ge(w_loaded, 16 * 5)
            nc.scalar.activation(wout_hi[:, :, :].rearrange("p q n -> p (q n)"), flat[:, 0:PAIRS * C],
                                 ACT.Copy).then_inc(w_hi_done, 1)
            for j in range(2, 2 * CK):
                split_x(0, j)
            act.wait_ge(vec_loaded, 16 * 8)
            act.wait_ge(consts_done, 4)
            seam(0, 0, False)
            attention(0, 0, HEAD2, False, True)
            with act.Fori(0, BATCH - 1) as b:
                attention(b, HEAD2, STEPS, True, True)
                seam(b, b + 1, True)
                attention(b + 1, 0, HEAD2, True, True)
            attention(BATCH - 1, HEAD2, STEPS, True, False)
            den(BATCH - 1, HEADS - 1, 1)
            for half in range(2):
                split_res(BATCH - 1, PAIRS - 1, half)
            for m in range(CK):
                add_gate(BATCH - 1, m)

        @block.vector
        def _(dve):
            flat = acc[:].rearrange("p k n -> p (k n)")
            chained = [0]

            def link(ins):
                chained[0] += 1
                ins.then_inc(set_chain, 1)
                dve.wait_ge(set_chain, chained[0])

            dve.wait_ge(vec_loaded, 16 * 8)
            nc.vector.tensor_scalar(tmp[:, 0, :], bn[:, 3, :], BN_EPS, None, ALU.add).then_inc(std_in, 1)
            dve.wait_ge(std_done, 1)
            link(nc.vector.reciprocal(tmp[:, 2, :], tmp[:, 1, :]))
            link(nc.vector.tensor_tensor(out=tmp[:, 1, :], in0=tmp[:, 2, :], in1=tmp[:, 2, :], op=ALU.mult))
            link(nc.vector.tensor_tensor(out=tmp[:, 1, :], in0=tmp[:, 1, :], in1=tmp[:, 0, :], op=ALU.mult))
            link(nc.vector.tensor_scalar(tmp[:, 1, :], tmp[:, 1, :], -0.5, 1.5, ALU.mult, ALU.add))
            link(nc.vector.tensor_tensor(out=tmp[:, 2, :], in0=tmp[:, 2, :], in1=tmp[:, 1, :], op=ALU.mult))
            link(nc.vector.tensor_tensor(out=bn_scale[:, :], in0=tmp[:, 2, :], in1=bn[:, 0, :], op=ALU.mult))
            link(nc.vector.tensor_tensor(out=tmp[:, 1, :], in0=bn_scale[:, :], in1=bn[:, 2, :], op=ALU.mult))
            link(nc.vector.tensor_tensor(out=bn_shift[:, :], in0=bn[:, 1, :], in1=tmp[:, 1, :], op=ALU.subtract))
            for part in range(2):
                dve.wait_ge(w_hi_done, part + 1)
                nc.vector.tensor_tensor(out=wqkv_lo[:, 2 * part:2 * part + 2, :].rearrange("p k n -> p (k n)"),
                                        in0=flat[:, 0:2 * 3 * C],
                                        in1=wqkv_hi[:, 2 * part:2 * part + 2, :].rearrange("p k n -> p (k n)").bitcast(F32),
                                        op=ALU.subtract).then_inc(w_lo_done, 1)
            dve.wait_ge(w_hi_done, 3)
            nc.vector.tensor_tensor(out=wout_lo[:, :, :].rearrange("p q n -> p (q n)"), in0=flat[:, 0:PAIRS * C],
                                    in1=wout_hi[:, :, :].rearrange("p q n -> p (q n)").bitcast(F32),
                                    op=ALU.subtract).then_inc(w_lo_done, 1)
            dve.wait_ge(tr_ps, 2)
            nc.vector.tensor_copy(guide_t[:, :, :].rearrange("p k r -> p (k r)"), ps_m[:, 0, :]).then_inc(tr_done, 1)
            nc.vector.tensor_copy(fuse_t[:, :], ps_m[:, 1, :]).then_inc(tr_done, 1)
            dve.wait_ge(b_ps, 1)
            nc.vector.tensor_tensor(out=b_res[:, :], in0=ps_p[:, 0:CK], in1=tmp[:, 3, :],
                                    op=ALU.add).then_inc(b_done, 1)

            def qk(b, h, half):
                dve.wait_ge(qk_hi_done, n_qk(b, 2 * h + half))
                cols = (h % 2, half_cols[half])
                nc.vector.scalar_tensor_tensor(out=q_both[(slice(DK, P), *cols)], in0=ps_p[0:DK, :],
                                               scalar=b_qk[0:DK, h:h + 1],
                                               in1=q_both[(slice(0, DK), *cols)].bitcast(F32),
                                               op0=ALU.add, op1=ALU.subtract)
                nc.vector.scalar_tensor_tensor(out=k_low[(slice(0, DK), *cols)], in0=ps_p[DK:P, :],
                                               scalar=b_qk[DK:P, h:h + 1],
                                               in1=k_twice[(slice(DK, P), *cols)].bitcast(F32),
                                               op0=ALU.add, op1=ALU.subtract).then_inc(qk_lo_done, 1)

            def v(b, kt):
                dve.wait_ge(v_hi_done, n_v(b, kt))
                cols = [t[:, kt, :].rearrange("p (h j) -> p h j", j=VW)[:, :, 0:DK] for t in (v_lo, v_hi)]
                nc.vector.tensor_tensor(out=cols[0],
                                        in0=ps_s[:, kt % SCORE_BANKS, :].rearrange("p (h j) -> p h j", j=DK),
                                        in1=cols[1].bitcast(F32), op=ALU.subtract).then_inc(v_lo_done, 1)

            def row_max(b, h, i):
                qt, kh = MAX_ORDER[i]
                dve.wait_ge(max_ps, n_max(b, h * 2 * KT + i))
                nc.vector.tensor_reduce(out=top_half[:, h % 2, qt, kh:kh + 1], in_=ps_m[:, i % 2, :],
                                        op=ALU.max, axis=AX_X).then_inc(max_done, 1)
                if i % KT == KT - 1:
                    half = i // KT
                    dve.wait_ge(max_done, n_max(b, h * 2 * KT + i))
                    nc.vector.tensor_reduce(out=top[:, h % 2, 4 * half:4 * half + 4],
                                            in_=top_half[:, h % 2, 4 * half:4 * half + 4, :],
                                            op=ALU.max, axis=AX_X).then_inc(top_done, 1)

            def out_add(b, p, half, m):
                i = out_i(p, half, m)
                dve.wait_ge(out_ps, n_out(b, i))
                if p == 0:
                    dve.wait_ge(acc_loaded[m], b * 16 + 16)
                else:
                    dve.wait_ge(out_done, n_out(b, i - 2 * CK))
                to = acc[:, m, half_cols[half]]
                if p < PAIRS - 1:
                    nc.vector.tensor_tensor(out=to, in0=ps_p[:, :], in1=to, op=ALU.add).then_inc(out_done, 1)
                else:
                    nc.vector.scalar_tensor_tensor(out=to, in0=ps_p[:, :], scalar=1.0, in1=to, op0=ALU.mult,
                                                   op1=ALU.add, accum_out=sums[:, m, half:half + 1]).then_inc(out_done, 1)

            def reciprocal(b, h, half):
                dve.wait_ge(den_spread, n_head_half_dma(b, 2 * h + half))
                nc.vector.reciprocal(rcp_sp[:, :], den_sp[:, :]).then_inc(rcp_done, 1)

            def normalise(b, h, half):
                dve.wait_ge(rcp_in, n_head_half_dma(b, 2 * h + half))
                nc.vector.tensor_tensor(out=res[rows(h), half, :], in0=ps_o[rows(h), half, :],
                                        in1=res[rows(h), half, :], op=ALU.mult).then_inc(norm_done, 1)

            def p_low(b, g):
                by_pool, n = lo_done(g)
                if not by_pool:
                    dve.wait_ge(p_raw_done, n_step(b, g))
                    if g >= LO_BUFS:
                        dve.wait_ge(pv_ps, n_step(b, g - LO_BUFS))
                    nc.vector.tensor_tensor(out=p_lo[:, g % LO_BUFS, :], in0=p_raw[:, g % RAW_BUFS, :],
                                            in1=p_hi[:, g % HI_BUFS, :].bitcast(F32),
                                            op=ALU.subtract).then_inc(p_lo_dve, 1)

            def attention(b, first, end, prev):
                for g in range(first, end):
                    h, u = divmod(g, UNITS)
                    if u - 1 in QK_AT and h + 1 < HEADS:
                        qk(b, h + 1, QK_AT[u - 1])
                    if g:
                        p_low(b, g - 1)
                    for item in beside(h, u):
                        if item[0] == "max":
                            row_max(b, item[1], item[2])
                        if item[0] == "out":
                            out_add(b, *item[1:])
                    for item in tail(h, u) if prev else []:
                        tail_item(b - 1, item)
                    if u == RCP_AT[0]:
                        reciprocal(b, h, 0)
                    if u == RCP_AT[1] and h:
                        reciprocal(b, h - 1, 1)
                    if u in NORM_AT and h:
                        normalise(b, h - 1, NORM_AT.index(u))
                if end == STEPS:
                    p_low(b, STEPS - 1)

            gate_links = 5

            def tail_item(b, item):
                def chain(ins, n):
                    ins.then_inc(gate_chain, 1)
                    dve.wait_ge(gate_chain, b * gate_links + n)

                if item[0] == "out":
                    out_add(b, *item[1:])
                if item == ("out", PAIRS - 1, 1, CK - 1):
                    dve.wait_ge(out_done, n_out(b, out_i(PAIRS - 1, 1, CK - 1)))
                    chain(nc.vector.tensor_tensor(out=y2[:, 0, :], in0=sums[:, :, 0], in1=sums[:, :, 1], op=ALU.add), 1)
                    nc.vector.scalar_tensor_tensor(out=avg[:, :], in0=y2[:, 0, :], scalar=1.0 / TOK, in1=b_res[:, :],
                                                   op0=ALU.mult, op1=ALU.add).then_inc(avg_done, 1)
                if item[0] == "gate1":
                    dve.wait_ge(gate1_ps, n_one(b, 0))
                    nc.vector.tensor_scalar(y1[:, :], ps_p[:, 0:1], 0.0, 6.0, ALU.max, ALU.min).then_inc(y1_done, 1)
                if item[0] == "gate2":
                    dve.wait_ge(gate2_ps, n_one(b, 0))
                    chain(nc.vector.tensor_tensor(out=y2[:, 1, :], in0=ps_p[:, 0:CK], in1=bn_scale[:, :], op=ALU.mult), 2)
                    chain(nc.vector.tensor_tensor(out=y2[:, 2, :], in0=y2[:, 1, :], in1=bn_shift[:, :], op=ALU.add), 3)
                    chain(nc.vector.tensor_scalar(y2[:, 1, :], y2[:, 2, :], 0.0, 6.0, ALU.max, ALU.min), 4)
                    chain(nc.vector.tensor_tensor(out=y2[:, 2, :], in0=y2[:, 1, :], in1=b_res[:, :], op=ALU.add), 5)
                    nc.vector.tensor_copy(y2[:, 3, :], y2[:, 2, :]).then_inc(y2_done, 1)

            def seam(b, nb, prev):
                if prev:
                    normalise(b, HEADS - 1, 0)
                kt = None
                for item in SEAM:
                    if item[0] in ("qk", "v", "max") and kt is not None:
                        v(nb, kt)
                        kt = None
                    if item[0] == "qk":
                        qk(nb, 0, item[1])
                    if item[0] == "v":
                        kt = item[1]
                    if item[0] == "max":
                        row_max(nb, 0, item[1])
                    if prev and item == ("v", 2):
                        reciprocal(b, HEADS - 1, 1)
                    if prev and item == ("v", 4):
                        normalise(b, HEADS - 1, 1)

            dve.wait_ge(consts_done, 4)
            seam(0, 0, False)
            attention(0, 0, HEAD2, False)
            with dve.Fori(0, BATCH - 1) as b:
                attention(b, HEAD2, STEPS, True)
                seam(b, b + 1, True)
                attention(b + 1, 0, HEAD2, True)
            attention(BATCH - 1, HEAD2, STEPS, True)
            normalise(BATCH - 1, HEADS - 1, 0)
            reciprocal(BATCH - 1, HEADS - 1, 1)
            normalise(BATCH - 1, HEADS - 1, 1)
            for item in TAIL:
                tail_item(BATCH - 1, item)

        @block.tensor
        def _(pe):
            flat = acc[:].rearrange("p k n -> p (k n)")
            mm = nc.tensor.matmul

            pe.wait_ge(consts_done, 5)
            pe.wait_ge(w_loaded, 16 * 5)
            pe.wait_ge(vec_loaded, 16 * 8)
            for k in range(CK):
                done = nc.tensor.transpose(ps_m[:, 0, k * P:(k + 1) * P], flat[:, 2048 + k * P:2048 + (k + 1) * P], ident[:, :])
            done.then_inc(tr_ps, 1)
            for k in range(CK):
                done = nc.tensor.transpose(ps_m[:, 1, k * P:(k + 1) * P], flat[:, 2560 + k * P:2560 + (k + 1) * P], ident[:, :])
            done.then_inc(tr_ps, 1)
            for m in range(CK):
                for q in range(PAIRS):
                    done = mm(ps_p[:, m:m + 1], flat[:, q * C + m * P:q * C + (m + 1) * P], b_v[:, q:q + 1],
                              start=(q == 0), stop=(q == PAIRS - 1))
            done.then_inc(b_ps, 1)

            def split3(to, pairs):
                n = 3 * len(pairs)
                i = 0
                for a_hi, a_lo, b_hi, b_lo in pairs:
                    for a, c in ((a_hi, b_hi), (a_hi, b_lo), (a_lo, b_hi)):
                        done = mm(to, a, c, start=(i == 0), stop=(i == n - 1))
                        i += 1
                return done

            def qk(b, h, half, free):
                free()
                if h == 0:
                    pe.wait_ge(x_lo_done, n_x(b, 2 * CK - 1))
                w, t = slice(h * QKV, h * QKV + P), half_cols[half]
                split3(ps_p[:, :], [(wqkv_hi[:, k, w], wqkv_lo[:, k, w], x_hi[:, k, t], x_lo[:, k, t])
                                    for k in range(CK)]).then_inc(qk_ps, 1)

            def v(b, kt, prev):
                if prev and kt < 2:
                    pe.wait_ge(p_raw_done, n_step(b - 1, STEPS - 2 + kt))
                if kt >= SCORE_BANKS:
                    pe.wait_ge(v_lo_done, n_v(b, kt - SCORE_BANKS))
                t = slice(kt * P, (kt + 1) * P)
                w_v = [w[:, :, :].rearrange("p k (h j) -> p k h j", j=QKV)[:, :, :, P:QKV] for w in (wqkv_hi, wqkv_lo)]
                split3(ps_s[:, kt % SCORE_BANKS, :], [(x_hi[:, k, t], x_lo[:, k, t], w_v[0][:, k], w_v[1][:, k])
                                                      for k in range(CK)]).then_inc(v_ps, 1)

            def row_max(b, h, i):
                qt, kh = MAX_ORDER[i]
                if i in (0, 4):
                    pe.wait_ge(qk_lo_done, n_qk(b, 2 * h + i // 4))
                    pe.wait_ge(k_in[i // 4], n_head_dma(b, h))
                if h or i >= 2:
                    pe.wait_ge(max_done, n_max(b, h * 2 * KT + i - 2))
                mm(ps_m[:, i % 2, :], q_both[:, h % 2, qt * P:(qt + 1) * P],
                   k_twice[:, h % 2, half_cols[kh]], start=True, stop=True).then_inc(max_ps, 1)

            def shift(b, h, half, free):
                free()
                pe.wait_ge(top_done, n_top(b, 2 * h + half))
                nc.tensor.transpose(ps_p[0:4, 0:P], top[:, h % 2, 4 * half:4 * half + 4],
                                    ident[:, :]).then_inc(shift_ps, 1)

            def out_proj(b, p, half, m, free):
                free()
                pe.wait_ge(res_lo_done, n_pair_half(b, 2 * p + half))
                w, t = slice(m * P, (m + 1) * P), half_cols[half]
                split3(ps_p[:, :], [(wout_hi[:, p, w], wout_lo[:, p, w], res_hi[:, t], res_lo[:, t])]).then_inc(out_ps, 1)

            def scores(b, g):
                h, u = divmod(g, UNITS)
                half, kt = divmod(u, KT)
                if g >= SCORE_BANKS:
                    pe.wait_ge(p_raw_done, n_step(b, g - SCORE_BANKS))
                else:
                    pe.wait_ge(v_lo_done, n_v(b, max(kt for kt in range(KT) if kt % SCORE_BANKS == g)))
                if kt == 0:
                    pe.wait_ge(shift_in[half], n_shift_dma(b, h))
                keys = slice(kt * P, (kt + 1) * P)
                to = ps_s[:, g % SCORE_BANKS, :]
                mm(to, k_twice[:, h % 2, keys], q_both[:, h % 2, half_cols[half]], start=True, stop=False)
                mm(to, k_low[0:DK + 1, h % 2, keys], q_shift[0:DK + 1, half, :],
                   start=False, stop=True).then_inc(score_ps, 1)

            def values(b, g, prev):
                h, u = divmod(g, UNITS)
                half, kt = divmod(u, KT)
                if kt == 0 and h:
                    pe.wait_ge(norm_done, n_head_half(b, 2 * (h - 1) + half))
                if kt == 0 and h == 0 and prev:
                    pe.wait_ge(norm_done, n_head_half(b - 1, 2 * (HEADS - 1) + half))
                at = h * VW if h % 2 == 0 else h * VW - DK
                cols = slice(at, at + P)
                to = ps_o[:, half, :]
                pe.wait_ge(p_hi_done, n_step(b, g))
                mm(to, v_hi[:, kt, cols], p_hi[:, g % HI_BUFS, :], start=(kt == 0), stop=False)
                mm(to, v_lo[:, kt, cols], p_hi[:, g % HI_BUFS, :], start=False, stop=False)
                by_pool, n = lo_done(g)
                if by_pool:
                    pe.wait_ge(p_lo_pool, b * LO_POOL + n)
                else:
                    pe.wait_ge(p_lo_dve, b * LO_DVE + n)
                mm(to, v_hi[:, kt, cols], p_lo[:, g % LO_BUFS, :], start=False, stop=(kt == KT - 1)).then_inc(pv_ps, 1)

            reader = [None]

            def free():
                if reader[0]:
                    pe.wait_ge(*reader[0])

            def shared(item, b):
                kind = item[0]
                if kind == "qk":
                    qk(b, item[1], item[2], free)
                    reader[0] = (qk_lo_done, n_qk(b, 2 * item[1] + item[2]))
                if kind == "shift":
                    shift(b, item[1], item[2], free)
                    reader[0] = (top_row_done, n_shift(b, 2 * item[1] + item[2]))
                if kind == "out":
                    out_proj(b, *item[1:], free)
                    reader[0] = (out_done, n_out(b, out_i(*item[1:])))

            def gate1(b):
                pe.wait_ge(avg_done, n_one(b, 0))
                for k in range(CK):
                    done = mm(ps_p[:, 0:1], guide_t[:, k, :], avg[:, k:k + 1], start=(k == 0), stop=(k == CK - 1))
                done.then_inc(gate1_ps, 1)

            def gate2(b):
                for m in range(CK):
                    done = mm(ps_p[:, m:m + 1], fuse_t[:, m * P:(m + 1) * P], y1[:, :], start=True, stop=True)
                done.then_inc(gate2_ps, 1)

            def tail_item(b, item):
                if item[0] == "out":
                    shared(item, b)
                if item[0] == "gate1":
                    free()
                    gate1(b)
                    reader[0] = (y1_done, n_one(b, 0))
                if item[0] == "gate2":
                    free()
                    gate2(b)
                    reader[0] = (y2_done, n_one(b, 0))

            def attention(b, first, end, prev):
                for g in range(first, end):
                    scores(b, g)
                    if g >= LAG:
                        values(b, g - LAG, prev)
                    h, u = divmod(g, UNITS)
                    for item in beside(h, u):
                        if item[0] == "max":
                            row_max(b, item[1], item[2])
                        else:
                            shared(item, b)
                    for item in tail(h, u) if prev else []:
                        tail_item(b - 1, item)

            def seam(b, nb, prev):
                for item in SEAM:
                    if item[0] == "qk":
                        shared(("qk", 0, item[1]), nb)
                    if item[0] == "v":
                        v(nb, item[1], prev)
                    if item[0] == "max":
                        row_max(nb, 0, item[1])
                    if item[0] == "shift":
                        shared(("shift", 0, 0), nb)
                    if prev and item[0] == "pv":
                        values(b, item[1], True)

            pe.wait_ge(w_lo_done, 3)
            pe.wait_ge(tr_done, 2)
            reader[0] = (b_done, 1)
            seam(0, 0, False)
            attention(0, 0, HEAD2, False)
            with pe.Fori(0, BATCH - 1) as b:
                reader[0] = (top_row_done, n_shift(b, 4))
                attention(b, HEAD2, STEPS, True)
                seam(b, b + 1, True)
                attention(b + 1, 0, HEAD2, True)
            reader[0] = (top_row_done, n_shift(BATCH - 1, 4))
            attention(BATCH - 1, HEAD2, STEPS, True)
            for g in range(STEPS - LAG, STEPS):
                values(BATCH - 1, g, True)
            for item in TAIL:
                tail_item(BATCH - 1, item)


_INS = ["x", "L0_conv_W_qkv", "L0_conv_b_qkv", "L0_conv_W_out", "L0_conv_b_out", "L1_conv_w_guide", "L1_conv_w_fuse",
        "L1_conv_bn_gamma", "L1_conv_bn_beta", "L1_conv_bn_mean", "L1_conv_bn_var"]
_OUTS = [((16, 512, 32, 32), "float32")]


def kernel(**inputs):
    import numpy as _np
    import concourse.bacc as _bacc
    from concourse import mybir as _mybir
    from concourse.bass_utils import run_bass_kernel_spmd as _run

    nc = _bacc.Bacc("TRN2", target_bir_lowering=False, num_devices=1, dynamic_dma_scratch_size=4096)
    arrays, args = {}, []
    for name in _INS:
        a = _np.ascontiguousarray(inputs[name])
        arrays[f"in_{name}_dram"] = a
        args.append(nc.dram_tensor(f"in_{name}_dram", a.shape, _mybir.dt.from_np(a.dtype), kind="ExternalInput").ap())
    for i, (shape, dtype) in enumerate(_OUTS):
        dt = _mybir.dt.from_np(_np.dtype(dtype))
        args.append(nc.dram_tensor(f"out_{i}_dram", shape, dt, kind="ExternalOutput").ap())
    attention_block_kernel(nc, *args)
    r = _run(nc, [arrays], core_ids=[0])
    return r.results[0]["out_0_dram"]
```

```python
from contextlib import ExitStack

import concourse.bass as bass
from concourse import mybir

P = 128
F32 = mybir.dt.float32
F32R = mybir.dt.float32r
ALU = mybir.AluOpType
ACT = mybir.ActivationFunctionType
AX_X = mybir.AxisListType.X

BATCH, C, TOK = 16, 512, 1024
HEADS, DK, RED = 8, 64, 128
CK = C // P
HALF = TOK // 2
KT = TOK // P
PAIRS = HEADS // 2
UNITS = 2 * KT
STEPS = HEADS * UNITS
QKV = 3 * DK
VW = DK + 1
LAG = 3
SCORE_BANKS, HI_BUFS, LO_BUFS, RAW_BUFS = 3, 4, 3, 3
SCALE = DK ** -0.5
BN_EPS = 1e-5

QK_AT = {0: 0, 3: 1}
MAX_ORDER = [(4 * half + qt, kh) for half in range(2) for kh in range(2) for qt in range(4)]
MAX_FROM = 3
MAX_LATE = MAX_FROM + len(MAX_ORDER) - UNITS
SHIFT1_AT, SHIFT0_AT = 5, 12
COPY1_AT, COPY0_AT = 1, 9
OUT_AT, LAST_OUT_AT = {7: 0, 9: 1, 11: 2, 14: 3}, {0: 0, 3: 1, 7: 2, 11: 3}
POOL_LO = (4, 7, 10, 13)
DEN_AT, RCP_AT, NORM_AT, RES_AT = (11, 3), (13, 5), (0, 8), (1, 9)
X_AT = {6: (5, 8, 11, 14), 7: (1, 6, 8, 11)}
X_AHEAD = 4

TAIL_OUT_AT = {6: (0, 0), 7: (0, 1), 8: (0, 2), 9: (0, 3), 10: (1, 0), 11: (1, 1), 13: (1, 2), 14: (1, 3)}
GATE_AT = {(1, 6): ("gate1",), (1, 7): ("gate2",)}
ADD_GATE_AT, STORE_AT, ACC_AT = (8, 9, 10, 11), (9, 10, 11, 12), (12, 13, 14, 15)
SET_UP_AT = {(0, 6): "guide", (0, 8): "fuse", (0, 10): "b_res"}
HEAD2 = 2 * UNITS

SEAM = [("qk", 0), ("pv", STEPS - 3), ("v", 0), ("pv", STEPS - 2), ("pv", STEPS - 1), ("v", 1), ("max", 0), ("max", 1),
        ("qk", 1), ("v", 2), ("max", 2), ("max", 3), ("v", 3), ("max", 4), ("max", 5), ("v", 4), ("max", 6),
        ("max", 7), ("v", 5), ("max", 8), ("shift",), ("max", 9), ("v", 6), ("max", 10), ("v", 7), ("max", 11),
        ("max", 12)]


def beside(h, u):
    items = []
    if u in QK_AT and h + 1 < HEADS:
        items.append(("qk", h + 1, QK_AT[u]))
    out_at = OUT_AT if h + 1 < HEADS else LAST_OUT_AT
    if u in out_at and h > 1:
        items.append(("out", h // 2 - 1, h % 2, out_at[u]))
    if u < MAX_LATE:
        items.append(("max", h, u + UNITS - MAX_FROM))
    if u >= MAX_FROM and h + 1 < HEADS:
        items.append(("max", h + 1, u - MAX_FROM))
    if u == SHIFT1_AT:
        items.append(("shift", h, 1))
    if u == SHIFT0_AT and h + 1 < HEADS:
        items.append(("shift", h + 1, 0))
    return items


def tail(h, u):
    items = []
    if h == 0 and u in TAIL_OUT_AT:
        items.append(("out", PAIRS - 1, *TAIL_OUT_AT[u]))
    if (h, u) in GATE_AT:
        items.append(GATE_AT[h, u])
    return items


TAIL = [i for h in range(2) for u in range(UNITS) for i in tail(h, u)]


def lo_done(g):
    pool = g % UNITS in POOL_LO
    return pool, sum((i % UNITS in POOL_LO) == pool for i in range(g + 1))


LO_POOL = HEADS * len(POOL_LO)
LO_DVE = STEPS - LO_POOL


def attention_block_kernel(nc, x, w_qkv, b_qkv, w_out, b_out, w_guide, w_fuse, gamma, beta, mean, var, out):
    x_v = x.rearrange("b (k p) h w -> b p k (h w)", p=P)
    out_v = out.rearrange("b (k p) h w -> b p k (h w)", p=P)
    wq_v = w_qkv.rearrange("(k p) n -> p k n", p=P)

    with ExitStack() as ctx:
        def sb(name, shape, dt=F32):
            return ctx.enter_context(nc.sbuf_tensor(name, shape, dt))

        def sem(name):
            return ctx.enter_context(nc.semaphore(name))

        wqkv_hi = sb("wqkv_hi", [P, CK, 3 * C], F32R)
        wqkv_lo = sb("wqkv_lo", [P, CK, 3 * C], F32R)
        wout_hi = sb("wout_hi", [P, PAIRS, C], F32R)
        wout_lo = sb("wout_lo", [P, PAIRS, C], F32R)
        x_hi = sb("x_hi", [P, CK, TOK], F32R)
        x_lo = sb("x_lo", [P, CK, TOK], F32R)
        x_raw = sb("x_raw", [P, 2, HALF])
        v_hi = sb("v_hi", [P, KT, HEADS * VW], F32R)
        v_lo = sb("v_lo", [P, KT, HEADS * VW], F32R)
        q_both = sb("q_both", [P, 2, TOK], F32R)
        k_twice = sb("k_twice", [P, 2, TOK], F32R)
        k_low = sb("k_low", [P, 2, TOK], F32R)
        q_shift = sb("q_shift", [P, 2, HALF], F32R)
        p_raw = sb("p_raw", [P, RAW_BUFS, HALF])
        p_hi = sb("p_hi", [P, HI_BUFS, HALF], F32R)
        p_lo = sb("p_lo", [P, LO_BUFS, HALF], F32R)
        acc = sb("acc", [P, CK, TOK])
        res_hi = sb("res_hi", [P, TOK], F32R)
        res_lo = sb("res_lo", [P, TOK], F32R)
        den_rows = sb("den_rows", [32, HALF])
        res = sb("res", [P, 2, HALF])
        den_sp = sb("den_sp", [P, HALF // P])
        rcp_sp = sb("rcp_sp", [P, HALF // P])
        top_half = sb("top_half", [P, 2, KT, 2])
        top = sb("top", [P, 2, KT])
        top_row = sb("top_row", [4, 2, P], F32R)
        ident = sb("ident", [P, P])
        guide_t = sb("guide_t", [P, CK, RED])
        fuse_t = sb("fuse_t", [P, C])
        b_qk = sb("b_qk", [P, HEADS])
        b_v = sb("b_v", [P, PAIRS])
        b_res = sb("b_res", [P, CK])
        bn = sb("bn", [P, 4, CK])
        bn_scale = sb("bn_scale", [P, CK])
        bn_shift = sb("bn_shift", [P, CK])
        tmp = sb("tmp", [P, 4, CK])
        sums = sb("sums", [P, CK, 2])
        avg = sb("avg", [P, CK])
        y1 = sb("y1", [P, 1])
        y2 = sb("y2", [P, 4, CK])
        rcp_dram = nc.dram_tensor("rcp_dram", [2, HALF], F32, kind="Internal").ap()

        ps_s = ctx.enter_context(nc.psum_tensor("ps_s", [P, SCORE_BANKS, HALF], F32))
        ps_o = ctx.enter_context(nc.psum_tensor("ps_o", [P, 2, HALF], F32))
        ps_m = ctx.enter_context(nc.psum_tensor("ps_m", [P, 2, HALF], F32))
        ps_p = ctx.enter_context(nc.psum_tensor("ps_p", [P, HALF], F32))

        w_loaded = [sem(f"w_loaded{k}") for k in range(CK + 1)]
        gate_loaded = sem("gate_loaded")
        first_x_loaded = [sem(f"first_x_loaded{k}") for k in range(CK)]
        w_hi_done = sem("w_hi_done")
        w_lo_done = sem("w_lo_done")
        vec_loaded = sem("vec_loaded")
        consts_done = sem("consts_done")
        tr_ps = sem("tr_ps")
        tr_done = sem("tr_done")
        b_ps = sem("b_ps")
        b_done = sem("b_done")
        std_in = sem("std_in")
        std_done = sem("std_done")
        set_chain = sem("set_chain")
        x_loaded = [sem("x_loaded0"), sem("x_loaded1")]
        x_hi_done = sem("x_hi_done")
        x_lo_done = sem("x_lo_done")
        acc_loaded = [sem(f"acc_loaded{m}") for m in range(CK)]
        qk_ps = sem("qk_ps")
        v_ps = sem("v_ps")
        max_ps = sem("max_ps")
        shift_ps = sem("shift_ps")
        score_ps = sem("score_ps")
        pv_ps = sem("pv_ps")
        out_ps = sem("out_ps")
        gate1_ps = sem("gate1_ps")
        gate2_ps = sem("gate2_ps")
        qk_hi_done = sem("qk_hi_done")
        v_hi_done = sem("v_hi_done")
        top_row_done = sem("top_row_done")
        p_hi_done = sem("p_hi_done")
        p_raw_done = sem("p_raw_done")
        den_done = sem("den_done")
        res_hi_done = sem("res_hi_done")
        qk_lo_done = sem("qk_lo_done")
        v_lo_done = sem("v_lo_done")
        max_done = sem("max_done")
        top_done = sem("top_done")
        p_lo_dve = sem("p_lo_dve")
        rcp_done = sem("rcp_done")
        norm_done = sem("norm_done")
        out_done = sem("out_done")
        avg_done = sem("avg_done")
        y1_done = sem("y1_done")
        y2_done = sem("y2_done")
        gate_chain = sem("gate_chain")
        y_done = sem("y_done")
        p_lo_pool = sem("p_lo_pool")
        res_lo_done = sem("res_lo_done")
        k_in = [sem("k_in0"), sem("k_in1")]
        shift_in = [sem("shift_in0"), sem("shift_in1")]
        den_spread = sem("den_spread")
        rcp_out = sem("rcp_out")
        rcp_in = sem("rcp_in")
        stored = [sem(f"stored{m}") for m in range(CK)]

        half_cols = [slice(0, HALF), slice(HALF, TOK)]

        def rows(h):
            return slice(DK * (h % 2), DK * (h % 2) + DK)

        def last(n, m=1):
            return lambda b, i: b * (n * m) + (i + 1) * m

        n_qk = n_shift = n_head_half = last(2 * HEADS)
        n_pair_half = last(2 * PAIRS)
        n_v = last(KT)
        n_max = last(HEADS * 2 * KT)
        n_top = last(2 * HEADS)
        n_step = last(STEPS)
        n_out = last(PAIRS * 2 * CK)
        n_one = last(1)
        n_x = last(2 * CK)
        n_x_dma = last(CK, 16)
        n_shift_dma = last(HEADS, 32)
        n_head_dma = last(HEADS, 16)
        n_head_half_dma = last(2 * HEADS, 16)
        out_i = lambda p, half, m: (p * 2 + half) * CK + m

        flat = acc[:, :, :].rearrange("p k n -> p (k n)")
        w_raw = [flat[:, 0:3 * C], flat[:, 3 * C:6 * C], p_raw[:, :, :].rearrange("p a n -> p (a n)"), flat[:, 0:3 * C]]
        wout_raw = flat[:, 3 * C:3 * C + PAIRS * C]
        first_x_raw = [flat[:, 6 * C:6 * C + TOK], x_raw[:, :, :].rearrange("p a n -> p (a n)")] * 2
        guide_raw, fuse_raw = res[:, 0, :], res[:, 1, :]

        last_banks = [ps_s[:, i, :] for i in range(SCORE_BANKS)] + [ps_p[:, :]]

        block = ctx.enter_context(nc.Block())

        @block.sync
        def _(sp):
            def load_acc(b, m):
                sp.dma_start(acc[:, m, :], x_v[b][:, m, :]).then_inc(acc_loaded[m], 16)

            def load_vectors():
                for i, vec in enumerate((gamma, beta, mean, var)):
                    sp.dma_start(bn[:, i, :], vec.rearrange("(k p) -> p k", p=P),
                                 allow_slow_non_contiguous=True).then_inc(vec_loaded, 16)
                sp.dma_start(tmp[:, 3, :], b_out.rearrange("(k p) -> p k", p=P),
                             allow_slow_non_contiguous=True).then_inc(vec_loaded, 16)
                sp.dma_start(b_qk[:, :], b_qkv.rearrange("(h j) -> j h", j=QKV)[0:P, :],
                             allow_slow_non_contiguous=True).then_inc(vec_loaded, 16)
                by_pair = b_qkv.rearrange("(q t j) -> t j q", t=2, j=QKV)
                for t in range(2):
                    sp.dma_start(b_v[rows(t), :], by_pair[t, P:QKV, :],
                                 allow_slow_non_contiguous=True).then_inc(vec_loaded, 16)

            for k in range(CK):
                if k >= 2:
                    sp.wait_ge(x_lo_done, 2 * (k - 1))
                sp.dma_start(first_x_raw[k], x_v[0][:, k, :]).then_inc(first_x_loaded[k], 16)
                if k == 3:
                    sp.wait_ge(w_lo_done, 1)
                sp.dma_start(w_raw[k], wq_v[:, k, :]).then_inc(w_loaded[k], 16)
                if k == 0:
                    load_vectors()
            sp.wait_ge(w_lo_done, 2)
            sp.wait_ge(x_lo_done, 6)
            sp.dma_start(wout_raw.rearrange("p (q n) -> p q n", q=PAIRS),
                         w_out.rearrange("(q p) n -> p q n", p=P)).then_inc(w_loaded[CK], 16)
            sp.dma_start(guide_raw, w_guide).then_inc(gate_loaded, 16)
            sp.dma_start(fuse_raw.rearrange("p (k r) -> p k r", k=CK),
                         w_fuse.rearrange("(k p) r -> p k r", p=P)).then_inc(gate_loaded, 16)

            def load_x(b, j):
                sp.wait_ge(x_lo_done, n_x(b, j - 2) if j > 1 else n_x(b - 1, 2 * CK - 2 + j))
                sp.dma_start(x_raw[:, j % 2, :], x_v[b][:, j // 2, half_cols[j % 2]]).then_inc(x_loaded[j % 2], 16)

            def twice(b, h, half):
                sp.wait_ge(qk_hi_done, n_qk(b, 2 * h + half))
                cols = (h % 2, half_cols[half])
                sp.dma_start(k_twice[(slice(0, DK), *cols)].bitcast(F32),
                             k_twice[(slice(DK, P), *cols)].bitcast(F32)).then_inc(k_in[half], 16)

            def copy_q(b, h, half):
                if h:
                    sp.wait_ge(score_ps, n_step(b, (h - 1) * UNITS + half * KT + KT - 1))
                sp.dma_start(q_shift[0:DK, half, :].bitcast(F32),
                             q_both[0:DK, h % 2, half_cols[half]].bitcast(F32)).then_inc(shift_in[half], 16)

            def shift_operand(b, h, half):
                sp.wait_ge(top_row_done, n_shift(b, 2 * h + half))
                sp.dma_start(q_shift[DK:DK + 1, half, :].bitcast(F32),
                             top_row[:, half, :].bitcast(F32)).then_inc(shift_in[half], 16)

            def spread_den(b, h, half):
                i = 2 * h + half
                sp.wait_ge(den_done, n_head_half(b, i))
                row = 0 if h % 2 == 0 else 31
                sp.dma_start(den_sp[:, :], den_rows[row:row + 1, :]).then_inc(den_spread, 16)

            def spread_rcp(b, h, half):
                i = 2 * h + half
                sp.wait_ge(rcp_done, n_head_half(b, i))
                sp.dma_start(rcp_dram[half].rearrange("(p a) -> p a", p=P), rcp_sp[:, :]).then_inc(rcp_out, 16)
                sp.wait_ge(rcp_out, n_head_half_dma(b, i))
                sp.dma_start(res[rows(h), half, :], rcp_dram[half].partition_broadcast(DK)).then_inc(rcp_in, 16)

            def store(b, m):
                sp.wait_ge(y_done, b * CK + m + 1)
                sp.dma_start(out_v[b][:, m, :], acc[:, m, :]).then_inc(stored[m], 16)

            def attention(b, first, end, prev, has_next):
                chunk = 0
                for g in range(first, end):
                    h, u = divmod(g, UNITS)
                    if u == COPY1_AT:
                        copy_q(b, h, 1)
                    if u == COPY0_AT and h + 1 < HEADS:
                        copy_q(b, h + 1, 0)
                    for item in beside(h, u):
                        if item[0] == "shift":
                            shift_operand(b, item[1], item[2])
                        if item[0] == "qk":
                            twice(b, item[1], item[2])
                    if u == DEN_AT[0]:
                        spread_den(b, h, 0)
                    if u == DEN_AT[1] and h:
                        spread_den(b, h - 1, 1)
                    if u == RCP_AT[0]:
                        spread_rcp(b, h, 0)
                    if u == RCP_AT[1] and h:
                        spread_rcp(b, h - 1, 1)
                    if prev and h == 1 and u in STORE_AT:
                        store(b - 1, STORE_AT.index(u))
                    if h == 1 and u in ACC_AT:
                        m = ACC_AT.index(u)
                        if prev:
                            sp.wait_ge(stored[m], b * 16)
                        elif m == 0:
                            sp.wait_ge(w_lo_done, CK + 1)
                            sp.wait_ge(b_ps, 1)
                        load_acc(b, m)
                    h_x, u_x = divmod(g + X_AHEAD, UNITS)
                    if has_next and u_x in X_AT.get(h_x, ()):
                        load_x(b + 1, chunk)
                        chunk += 1

            def seam(b):
                for item in SEAM:
                    if item[0] == "qk":
                        twice(b + 1, 0, item[1])
                        if item[1] == 0:
                            copy_q(b + 1, 0, 0)
                    if item == ("pv", STEPS - 1):
                        spread_den(b, HEADS - 1, 1)
                    if item == ("v", 2):
                        spread_rcp(b, HEADS - 1, 1)
                    if item[0] == "shift":
                        shift_operand(b + 1, 0, 0)

            for half in range(2):
                twice(0, 0, half)
            copy_q(0, 0, 0)
            shift_operand(0, 0, 0)
            attention(0, 0, HEAD2, False, True)
            with sp.Fori(0, BATCH - 1) as b:
                attention(b, HEAD2, STEPS, True, True)
                seam(b)
                attention(b + 1, 0, HEAD2, True, True)
            attention(BATCH - 1, HEAD2, STEPS, True, False)
            spread_den(BATCH - 1, HEADS - 1, 1)
            spread_rcp(BATCH - 1, HEADS - 1, 1)
            for m in range(CK):
                store(BATCH - 1, m)
            for m in range(CK):
                sp.wait_ge(stored[m], BATCH * 16)

        @block.gpsimd
        def _(pool):
            nc.gpsimd.memset(ident[:, :], 0.0).then_inc(consts_done, 1)
            nc.gpsimd.memset(v_hi[:, :, :].bitcast(F32), 1.0).then_inc(consts_done, 1)
            nc.gpsimd.memset(v_lo[:, :, :].bitcast(F32), 0.0).then_inc(consts_done, 1)
            pool.wait_ge(consts_done, 3)
            nc.gpsimd.memset(k_low[DK:P, :, :].bitcast(F32), 1.0).then_inc(consts_done, 1)
            pool.wait_ge(consts_done, 4)
            nc.gpsimd.affine_select(out=ident[:, :], in_=ident[:, :], compare_op=ALU.not_equal, fill=1.0,
                                    base=0, pattern=[[-1, P]], channel_multiplier=1).then_inc(consts_done, 1)

            def split_x(b, j, first=False):
                pool.wait_ge(x_hi_done, n_x(b, j))
                cols = (slice(None), j // 2, half_cols[j % 2])
                raw = first_x_raw[j // 2][:, half_cols[j % 2]] if first else x_raw[:, j % 2, :]
                nc.gpsimd.tensor_tensor(out=x_lo[cols], in0=raw, in1=x_hi[cols].bitcast(F32),
                                        op=ALU.subtract).then_inc(x_lo_done, 1)

            def split_res(b, p, half):
                pool.wait_ge(res_hi_done, n_pair_half(b, 2 * p + half))
                nc.gpsimd.tensor_tensor(out=res_lo[:, half_cols[half]], in0=res[:, half, :],
                                        in1=res_hi[:, half_cols[half]].bitcast(F32),
                                        op=ALU.subtract).then_inc(res_lo_done, 1)

            def attention(b, first, end, has_next):
                chunk = 0
                for g in range(first, end):
                    h, u = divmod(g, UNITS)
                    if lo_done(g)[0]:
                        pool.wait_ge(p_raw_done, n_step(b, g))
                        if g >= LO_BUFS:
                            pool.wait_ge(pv_ps, n_step(b, g - LO_BUFS))
                        nc.gpsimd.tensor_tensor(out=p_lo[:, g % LO_BUFS, :], in0=p_raw[:, g % RAW_BUFS, :],
                                                in1=p_hi[:, g % HI_BUFS, :].bitcast(F32),
                                                op=ALU.subtract).then_inc(p_lo_pool, 1)
                    if h and h % 2 == 0 and u in RES_AT:
                        split_res(b, h // 2 - 1, RES_AT.index(u))
                    if has_next and h in X_AT and u in X_AT[h]:
                        split_x(b + 1, chunk)
                        chunk += 1

            def end(b):
                split_res(b, PAIRS - 1, 0)
                split_res(b, PAIRS - 1, 1)

            for j in range(2 * CK):
                split_x(0, j, True)
            attention(0, 0, HEAD2, True)
            with pool.Fori(0, BATCH - 1) as b:
                attention(b, HEAD2, STEPS, True)
                end(b)
                attention(b + 1, 0, HEAD2, True)
            attention(BATCH - 1, HEAD2, STEPS, False)
            end(BATCH - 1)

        @block.scalar
        def _(act):
            def split_x(b, j, first=False):
                cols = (slice(None), j // 2, half_cols[j % 2])
                if first:
                    act.wait_ge(first_x_loaded[j // 2], 16)
                else:
                    act.wait_ge(x_loaded[j % 2], n_x_dma(b - 1, j // 2))
                nc.scalar.activation(x_hi[cols], first_x_raw[j // 2][:, half_cols[j % 2]] if first else x_raw[:, j % 2, :],
                                     ACT.Copy).then_inc(x_hi_done, 1)

            def qk(b, h, half):
                act.wait_ge(qk_ps, n_qk(b, 2 * h + half))
                cols = (h % 2, half_cols[half])
                nc.scalar.activation(q_both[(slice(0, DK), *cols)], ps_p[0:DK, :], ACT.Identity,
                                     bias=b_qk[0:DK, h:h + 1])
                nc.scalar.activation(k_twice[(slice(DK, P), *cols)], ps_p[DK:P, :], ACT.Identity,
                                     bias=b_qk[DK:P, h:h + 1]).then_inc(qk_hi_done, 1)

            def v(b, kt):
                act.wait_ge(v_ps, n_v(b, kt))
                nc.scalar.activation(v_hi[:, kt, :].rearrange("p (h j) -> p h j", j=VW)[:, :, 0:DK],
                                     ps_s[:, kt % SCORE_BANKS, :].rearrange("p (h j) -> p h j", j=DK),
                                     ACT.Copy).then_inc(v_hi_done, 1)

            def shift(b, h, half):
                act.wait_ge(shift_ps, n_shift(b, 2 * h + half))
                if h:
                    act.wait_ge(shift_in[half], n_shift_dma(b, h - 1))
                nc.scalar.activation(top_row[:, half, :], ps_p[0:4, 0:P], ACT.Copy,
                                     scale=-1.0).then_inc(top_row_done, 1)

            def den(b, h, half):
                i = 2 * h + half
                act.wait_ge(pv_ps, n_step(b, h * UNITS + half * KT + KT - 1))
                if i:
                    act.wait_ge(den_spread, n_head_half_dma(b, i - 1))
                at = DK if h % 2 == 0 else DK - 32
                nc.scalar.activation(den_rows[:, :], ps_o[at:at + 32, half, :], ACT.Copy).then_inc(den_done, 1)

            def split_res(b, p, half):
                act.wait_ge(norm_done, n_head_half(b, 2 * (2 * p + 1) + half))
                if p:
                    act.wait_ge(out_ps, n_out(b, out_i(p - 1, half, CK - 1)))
                nc.scalar.activation(res_hi[:, half_cols[half]], res[:, half, :],
                                     ACT.Copy).then_inc(res_hi_done, 1)

            def attention(b, first, end, prev, has_next):
                chunk = 0
                for g in range(first, end):
                    h, u = divmod(g, UNITS)
                    act.wait_ge(score_ps, n_step(b, g))
                    if g >= HI_BUFS:
                        act.wait_ge(pv_ps, n_step(b, g - HI_BUFS))
                    nc.scalar.activation(p_hi[:, g % HI_BUFS, :], ps_s[:, g % SCORE_BANKS, :], ACT.Exp,
                                         scale=SCALE).then_inc(p_hi_done, 1)
                    if g >= RAW_BUFS:
                        by_pool, n = lo_done(g - RAW_BUFS)
                        if by_pool:
                            act.wait_ge(p_lo_pool, b * LO_POOL + n)
                        else:
                            act.wait_ge(p_lo_dve, b * LO_DVE + n)
                    nc.scalar.activation(p_raw[:, g % RAW_BUFS, :], ps_s[:, g % SCORE_BANKS, :], ACT.Exp,
                                         scale=SCALE).then_inc(p_raw_done, 1)
                    for item in beside(h, u):
                        if item[0] == "qk":
                            qk(b, item[1], item[2])
                        if item[0] == "shift":
                            shift(b, item[1], item[2])
                    if u == DEN_AT[0]:
                        den(b, h, 0)
                    if u == DEN_AT[1] and h:
                        den(b, h - 1, 1)
                    if u in RES_AT and h and h % 2 == 0:
                        split_res(b, h // 2 - 1, RES_AT.index(u))
                    if has_next and h in X_AT and u in X_AT[h]:
                        if chunk == 0:
                            act.wait_ge(qk_ps, n_qk(b, 2 * HEADS - 1))
                        split_x(b + 1, chunk)
                        chunk += 1

            def seam(b, nb, prev):
                for item in SEAM:
                    if item[0] == "qk":
                        qk(nb, 0, item[1])
                    if item[0] == "v":
                        v(nb, item[1])
                    if item[0] == "shift":
                        shift(nb, 0, 0)
                    if prev and item == ("pv", STEPS - 1):
                        den(b, HEADS - 1, 1)
                    if prev and item == ("v", 1):
                        split_res(b, PAIRS - 1, 0)
                    if prev and item == ("v", 5):
                        split_res(b, PAIRS - 1, 1)

            for k in range(CK):
                for half in range(2):
                    split_x(0, 2 * k + half, True)
                act.wait_ge(w_loaded[k], 16)
                nc.scalar.activation(wqkv_hi[:, k, :], w_raw[k], ACT.Copy).then_inc(w_hi_done, 1)
            act.wait_ge(std_in, 1)
            nc.scalar.activation(tmp[:, 1, :], tmp[:, 0, :], ACT.Sqrt).then_inc(std_done, 1)
            act.wait_ge(w_loaded[CK], 16)
            nc.scalar.activation(wout_hi[:, :, :].rearrange("p q n -> p (q n)"), wout_raw,
                                 ACT.Copy).then_inc(w_hi_done, 1)
            act.wait_ge(vec_loaded, 16 * 8)
            act.wait_ge(consts_done, 4)
            seam(0, 0, False)
            attention(0, 0, HEAD2, False, True)
            with act.Fori(0, BATCH - 1) as b:
                attention(b, HEAD2, STEPS, True, True)
                seam(b, b + 1, True)
                attention(b + 1, 0, HEAD2, True, True)
            attention(BATCH - 1, HEAD2, STEPS, True, False)
            den(BATCH - 1, HEADS - 1, 1)
            for half in range(2):
                split_res(BATCH - 1, PAIRS - 1, half)

        @block.vector
        def _(dve):
            chained = [0]

            def link(ins):
                chained[0] += 1
                ins.then_inc(set_chain, 1)
                dve.wait_ge(set_chain, chained[0])

            dve.wait_ge(vec_loaded, 16 * 8)
            nc.vector.tensor_scalar(tmp[:, 0, :], bn[:, 3, :], BN_EPS, None, ALU.add).then_inc(std_in, 1)
            for k in range(CK):
                dve.wait_ge(w_hi_done, k + 1)
                nc.vector.tensor_tensor(out=wqkv_lo[:, k, :], in0=w_raw[k], in1=wqkv_hi[:, k, :].bitcast(F32),
                                        op=ALU.subtract).then_inc(w_lo_done, 1)
            dve.wait_ge(std_done, 1)
            link(nc.vector.reciprocal(tmp[:, 2, :], tmp[:, 1, :]))
            link(nc.vector.tensor_tensor(out=tmp[:, 1, :], in0=tmp[:, 2, :], in1=tmp[:, 2, :], op=ALU.mult))
            link(nc.vector.tensor_tensor(out=tmp[:, 1, :], in0=tmp[:, 1, :], in1=tmp[:, 0, :], op=ALU.mult))
            link(nc.vector.tensor_scalar(tmp[:, 1, :], tmp[:, 1, :], -0.5, 1.5, ALU.mult, ALU.add))
            link(nc.vector.tensor_tensor(out=tmp[:, 2, :], in0=tmp[:, 2, :], in1=tmp[:, 1, :], op=ALU.mult))
            link(nc.vector.tensor_tensor(out=bn_scale[:, :], in0=tmp[:, 2, :], in1=bn[:, 0, :], op=ALU.mult))
            link(nc.vector.tensor_tensor(out=tmp[:, 1, :], in0=bn_scale[:, :], in1=bn[:, 2, :], op=ALU.mult))
            link(nc.vector.tensor_tensor(out=bn_shift[:, :], in0=bn[:, 1, :], in1=tmp[:, 1, :], op=ALU.subtract))
            dve.wait_ge(w_hi_done, CK + 1)
            nc.vector.tensor_tensor(out=wout_lo[:, :, :].rearrange("p q n -> p (q n)"),
                                    in0=wout_raw,
                                    in1=wout_hi[:, :, :].rearrange("p q n -> p (q n)").bitcast(F32),
                                    op=ALU.subtract).then_inc(w_lo_done, 1)

            def set_up(what):
                if what == "guide":
                    dve.wait_ge(tr_ps, 1)
                    nc.vector.tensor_copy(guide_t[:, :, :].rearrange("p k r -> p (k r)"), ps_p[:, :]).then_inc(tr_done, 1)
                if what == "fuse":
                    dve.wait_ge(tr_ps, 2)
                    nc.vector.tensor_copy(fuse_t[:, :], ps_p[:, :]).then_inc(tr_done, 1)
                if what == "b_res":
                    dve.wait_ge(b_ps, 1)
                    nc.vector.tensor_tensor(out=b_res[:, :], in0=ps_p[:, 0:CK], in1=tmp[:, 3, :],
                                            op=ALU.add).then_inc(b_done, 1)

            def qk(b, h, half):
                dve.wait_ge(qk_hi_done, n_qk(b, 2 * h + half))
                cols = (h % 2, half_cols[half])
                nc.vector.scalar_tensor_tensor(out=q_both[(slice(DK, P), *cols)], in0=ps_p[0:DK, :],
                                               scalar=b_qk[0:DK, h:h + 1],
                                               in1=q_both[(slice(0, DK), *cols)].bitcast(F32),
                                               op0=ALU.add, op1=ALU.subtract)
                nc.vector.scalar_tensor_tensor(out=k_low[(slice(0, DK), *cols)], in0=ps_p[DK:P, :],
                                               scalar=b_qk[DK:P, h:h + 1],
                                               in1=k_twice[(slice(DK, P), *cols)].bitcast(F32),
                                               op0=ALU.add, op1=ALU.subtract).then_inc(qk_lo_done, 1)

            def v(b, kt):
                dve.wait_ge(v_hi_done, n_v(b, kt))
                cols = [t[:, kt, :].rearrange("p (h j) -> p h j", j=VW)[:, :, 0:DK] for t in (v_lo, v_hi)]
                nc.vector.tensor_tensor(out=cols[0],
                                        in0=ps_s[:, kt % SCORE_BANKS, :].rearrange("p (h j) -> p h j", j=DK),
                                        in1=cols[1].bitcast(F32), op=ALU.subtract).then_inc(v_lo_done, 1)

            def row_max(b, h, i):
                qt, kh = MAX_ORDER[i]
                dve.wait_ge(max_ps, n_max(b, h * 2 * KT + i))
                nc.vector.tensor_reduce(out=top_half[:, h % 2, qt, kh:kh + 1], in_=ps_m[:, i % 2, :],
                                        op=ALU.max, axis=AX_X).then_inc(max_done, 1)
                if i % KT == KT - 1:
                    half = i // KT
                    dve.wait_ge(max_done, n_max(b, h * 2 * KT + i))
                    nc.vector.tensor_reduce(out=top[:, h % 2, 4 * half:4 * half + 4],
                                            in_=top_half[:, h % 2, 4 * half:4 * half + 4, :],
                                            op=ALU.max, axis=AX_X).then_inc(top_done, 1)

            def out_add(b, p, half, m, bank=ps_p[:, :]):
                i = out_i(p, half, m)
                dve.wait_ge(out_ps, n_out(b, i))
                if p == 0:
                    dve.wait_ge(acc_loaded[m], b * 16 + 16)
                else:
                    dve.wait_ge(out_done, n_out(b, i - 2 * CK))
                to = acc[:, m, half_cols[half]]
                if p < PAIRS - 1:
                    nc.vector.tensor_tensor(out=to, in0=bank, in1=to, op=ALU.add).then_inc(out_done, 1)
                else:
                    nc.vector.scalar_tensor_tensor(out=to, in0=bank, scalar=1.0, in1=to, op0=ALU.mult,
                                                   op1=ALU.add, accum_out=sums[:, m, half:half + 1]).then_inc(out_done, 1)

            def reciprocal(b, h, half):
                dve.wait_ge(den_spread, n_head_half_dma(b, 2 * h + half))
                nc.vector.reciprocal(rcp_sp[:, :], den_sp[:, :]).then_inc(rcp_done, 1)

            def normalise(b, h, half):
                dve.wait_ge(rcp_in, n_head_half_dma(b, 2 * h + half))
                nc.vector.tensor_tensor(out=res[rows(h), half, :], in0=ps_o[rows(h), half, :],
                                        in1=res[rows(h), half, :], op=ALU.mult).then_inc(norm_done, 1)

            def p_low(b, g):
                by_pool, n = lo_done(g)
                if not by_pool:
                    dve.wait_ge(p_raw_done, n_step(b, g))
                    if g >= LO_BUFS:
                        dve.wait_ge(pv_ps, n_step(b, g - LO_BUFS))
                    nc.vector.tensor_tensor(out=p_lo[:, g % LO_BUFS, :], in0=p_raw[:, g % RAW_BUFS, :],
                                            in1=p_hi[:, g % HI_BUFS, :].bitcast(F32),
                                            op=ALU.subtract).then_inc(p_lo_dve, 1)

            def attention(b, first, end, prev):
                for g in range(first, end):
                    h, u = divmod(g, UNITS)
                    if g and u == 1:
                        p_low(b, g - 1)
                    if u - 1 in QK_AT and h + 1 < HEADS:
                        qk(b, h + 1, QK_AT[u - 1])
                    if g and u != 1:
                        p_low(b, g - 1)
                    for item in beside(h, u):
                        if item[0] == "max":
                            row_max(b, item[1], item[2])
                        if item[0] == "out":
                            out_add(b, *item[1:])
                    for item in tail(h, u) if prev else []:
                        tail_item(b - 1, item)
                    if not prev and (h, u) in SET_UP_AT:
                        set_up(SET_UP_AT[h, u])
                    if prev and h == 1 and u in ADD_GATE_AT:
                        add_gate(b - 1, ADD_GATE_AT.index(u))
                    if u == RCP_AT[0]:
                        reciprocal(b, h, 0)
                    if u == RCP_AT[1] and h:
                        reciprocal(b, h - 1, 1)
                    if u in NORM_AT and h:
                        normalise(b, h - 1, NORM_AT.index(u))
                if end == STEPS:
                    p_low(b, STEPS - 1)

            gate_links = 5

            def tail_item(b, item, bank=ps_p[:, :]):
                def chain(ins, n):
                    ins.then_inc(gate_chain, 1)
                    dve.wait_ge(gate_chain, b * gate_links + n)

                if item[0] == "out":
                    out_add(b, *item[1:], bank)
                if item == ("out", PAIRS - 1, 1, CK - 1):
                    dve.wait_ge(out_done, n_out(b, out_i(PAIRS - 1, 1, CK - 1)))
                    chain(nc.vector.tensor_tensor(out=y2[:, 0, :], in0=sums[:, :, 0], in1=sums[:, :, 1], op=ALU.add), 1)
                    nc.vector.scalar_tensor_tensor(out=avg[:, :], in0=y2[:, 0, :], scalar=1.0 / TOK, in1=b_res[:, :],
                                                   op0=ALU.mult, op1=ALU.add).then_inc(avg_done, 1)
                if item[0] == "gate1":
                    dve.wait_ge(gate1_ps, n_one(b, 0))
                    nc.vector.tensor_scalar(y1[:, :], ps_p[:, 0:1], 0.0, 6.0, ALU.max, ALU.min).then_inc(y1_done, 1)
                if item[0] == "gate2":
                    dve.wait_ge(gate2_ps, n_one(b, 0))
                    chain(nc.vector.tensor_tensor(out=y2[:, 1, :], in0=ps_p[:, 0:CK], in1=bn_scale[:, :], op=ALU.mult), 2)
                    chain(nc.vector.tensor_tensor(out=y2[:, 2, :], in0=y2[:, 1, :], in1=bn_shift[:, :], op=ALU.add), 3)
                    chain(nc.vector.tensor_scalar(y2[:, 1, :], y2[:, 2, :], 0.0, 6.0, ALU.max, ALU.min), 4)
                    chain(nc.vector.tensor_tensor(out=y2[:, 2, :], in0=y2[:, 1, :], in1=b_res[:, :], op=ALU.add), 5)
                    nc.vector.tensor_copy(y2[:, 3, :], y2[:, 2, :]).then_inc(y2_done, 1)

            def add_gate(b, m):
                dve.wait_ge(y2_done, n_one(b, 0))
                nc.vector.tensor_scalar(acc[:, m, :], acc[:, m, :], y2[:, 3, m:m + 1], None,
                                        ALU.add).then_inc(y_done, 1)

            def seam(b, nb, prev):
                if prev:
                    normalise(b, HEADS - 1, 0)
                kt = None
                for item in SEAM:
                    if item[0] in ("qk", "v", "max") and kt is not None:
                        v(nb, kt)
                        kt = None
                    if item[0] == "qk":
                        qk(nb, 0, item[1])
                    if item[0] == "v":
                        kt = item[1]
                    if item[0] == "max":
                        row_max(nb, 0, item[1])
                    if prev and item == ("v", 2):
                        reciprocal(b, HEADS - 1, 1)
                    if prev and item == ("v", 4):
                        normalise(b, HEADS - 1, 1)

            dve.wait_ge(consts_done, 4)
            seam(0, 0, False)
            attention(0, 0, HEAD2, False)
            with dve.Fori(0, BATCH - 1) as b:
                attention(b, HEAD2, STEPS, True)
                seam(b, b + 1, True)
                attention(b + 1, 0, HEAD2, True)
            attention(BATCH - 1, HEAD2, STEPS, True)
            normalise(BATCH - 1, HEADS - 1, 0)
            reciprocal(BATCH - 1, HEADS - 1, 1)
            for i, item in enumerate(TAIL):
                if item == ("out", PAIRS - 1, 1, 0):
                    normalise(BATCH - 1, HEADS - 1, 1)
                tail_item(BATCH - 1, item, last_banks[i % len(last_banks)])
            for m in range(CK):
                add_gate(BATCH - 1, m)

        @block.tensor
        def _(pe):
            mm = nc.tensor.matmul

            def set_up(what):
                free()
                if what in ("guide", "fuse"):
                    pe.wait_ge(gate_loaded, 32)
                    raw = guide_raw if what == "guide" else fuse_raw
                    for k in range(CK):
                        done = nc.tensor.transpose(ps_p[:, k * P:(k + 1) * P], raw[:, k * P:(k + 1) * P], ident[:, :])
                    done.then_inc(tr_ps, 1)
                    reader[0] = (tr_done, 1 if what == "guide" else 2)
                else:
                    pe.wait_ge(w_loaded[CK], 16)
                    for m in range(CK):
                        for q in range(PAIRS):
                            done = mm(ps_p[:, m:m + 1], wout_raw[:, q * C + m * P:q * C + (m + 1) * P], b_v[:, q:q + 1],
                                      start=(q == 0), stop=(q == PAIRS - 1))
                    done.then_inc(b_ps, 1)
                    reader[0] = (b_done, 1)

            def split3(to, pairs):
                n = 3 * len(pairs)
                i = 0
                for a_hi, a_lo, b_hi, b_lo in pairs:
                    for a, c in ((a_hi, b_hi), (a_hi, b_lo), (a_lo, b_hi)):
                        done = mm(to, a, c, start=(i == 0), stop=(i == n - 1))
                        i += 1
                return done

            def qk(b, h, half, free):
                free()
                if h == 0:
                    pe.wait_ge(x_lo_done, n_x(b, 2 * CK - 1))
                w, t = slice(h * QKV, h * QKV + P), half_cols[half]
                split3(ps_p[:, :], [(wqkv_hi[:, k, w], wqkv_lo[:, k, w], x_hi[:, k, t], x_lo[:, k, t])
                                    for k in range(CK)]).then_inc(qk_ps, 1)

            def v(b, kt, prev):
                if prev and kt < 2:
                    pe.wait_ge(p_raw_done, n_step(b - 1, STEPS - 2 + kt))
                if kt >= SCORE_BANKS:
                    pe.wait_ge(v_lo_done, n_v(b, kt - SCORE_BANKS))
                t = slice(kt * P, (kt + 1) * P)
                w_v = [w[:, :, :].rearrange("p k (h j) -> p k h j", j=QKV)[:, :, :, P:QKV] for w in (wqkv_hi, wqkv_lo)]
                split3(ps_s[:, kt % SCORE_BANKS, :], [(x_hi[:, k, t], x_lo[:, k, t], w_v[0][:, k], w_v[1][:, k])
                                                      for k in range(CK)]).then_inc(v_ps, 1)

            def row_max(b, h, i):
                qt, kh = MAX_ORDER[i]
                if i in (0, 4):
                    pe.wait_ge(qk_lo_done, n_qk(b, 2 * h + i // 4))
                    pe.wait_ge(k_in[i // 4], n_head_dma(b, h))
                if h or i >= 2:
                    pe.wait_ge(max_done, n_max(b, h * 2 * KT + i - 2))
                mm(ps_m[:, i % 2, :], q_both[:, h % 2, qt * P:(qt + 1) * P],
                   k_twice[:, h % 2, half_cols[kh]], start=True, stop=True).then_inc(max_ps, 1)

            def shift(b, h, half, free):
                free()
                pe.wait_ge(top_done, n_top(b, 2 * h + half))
                nc.tensor.transpose(ps_p[0:4, 0:P], top[:, h % 2, 4 * half:4 * half + 4],
                                    ident[:, :]).then_inc(shift_ps, 1)

            def out_proj(b, p, half, m, free, bank=ps_p[:, :]):
                free()
                pe.wait_ge(res_lo_done, n_pair_half(b, 2 * p + half))
                w, t = slice(m * P, (m + 1) * P), half_cols[half]
                split3(bank, [(wout_hi[:, p, w], wout_lo[:, p, w], res_hi[:, t], res_lo[:, t])]).then_inc(out_ps, 1)

            def scores(b, g):
                h, u = divmod(g, UNITS)
                half, kt = divmod(u, KT)
                if g >= SCORE_BANKS:
                    pe.wait_ge(p_raw_done, n_step(b, g - SCORE_BANKS))
                else:
                    pe.wait_ge(v_lo_done, n_v(b, max(kt for kt in range(KT) if kt % SCORE_BANKS == g)))
                if kt == 0:
                    pe.wait_ge(shift_in[half], n_shift_dma(b, h))
                keys = slice(kt * P, (kt + 1) * P)
                to = ps_s[:, g % SCORE_BANKS, :]
                mm(to, k_twice[:, h % 2, keys], q_both[:, h % 2, half_cols[half]], start=True, stop=False)
                mm(to, k_low[0:DK + 1, h % 2, keys], q_shift[0:DK + 1, half, :],
                   start=False, stop=True).then_inc(score_ps, 1)

            def values(b, g, prev):
                h, u = divmod(g, UNITS)
                half, kt = divmod(u, KT)
                if kt == 0 and h:
                    pe.wait_ge(norm_done, n_head_half(b, 2 * (h - 1) + half))
                if kt == 0 and h == 0 and prev:
                    pe.wait_ge(norm_done, n_head_half(b - 1, 2 * (HEADS - 1) + half))
                at = h * VW if h % 2 == 0 else h * VW - DK
                cols = slice(at, at + P)
                to = ps_o[:, half, :]
                pe.wait_ge(p_hi_done, n_step(b, g))
                mm(to, v_hi[:, kt, cols], p_hi[:, g % HI_BUFS, :], start=(kt == 0), stop=False)
                mm(to, v_lo[:, kt, cols], p_hi[:, g % HI_BUFS, :], start=False, stop=False)
                by_pool, n = lo_done(g)
                if by_pool:
                    pe.wait_ge(p_lo_pool, b * LO_POOL + n)
                else:
                    pe.wait_ge(p_lo_dve, b * LO_DVE + n)
                mm(to, v_hi[:, kt, cols], p_lo[:, g % LO_BUFS, :], start=False, stop=(kt == KT - 1)).then_inc(pv_ps, 1)

            reader = [None]

            def free():
                if reader[0]:
                    pe.wait_ge(*reader[0])

            def shared(item, b):
                kind = item[0]
                if kind == "qk":
                    qk(b, item[1], item[2], free)
                    reader[0] = (qk_lo_done, n_qk(b, 2 * item[1] + item[2]))
                if kind == "shift":
                    shift(b, item[1], item[2], free)
                    reader[0] = (top_row_done, n_shift(b, 2 * item[1] + item[2]))
                if kind == "out":
                    out_proj(b, *item[1:], free)
                    reader[0] = (out_done, n_out(b, out_i(*item[1:])))

            def gate1(b):
                pe.wait_ge(avg_done, n_one(b, 0))
                for k in range(CK):
                    done = mm(ps_p[:, 0:1], guide_t[:, k, :], avg[:, k:k + 1], start=(k == 0), stop=(k == CK - 1))
                done.then_inc(gate1_ps, 1)

            def gate2(b):
                for m in range(CK):
                    done = mm(ps_p[:, m:m + 1], fuse_t[:, m * P:(m + 1) * P], y1[:, :], start=True, stop=True)
                done.then_inc(gate2_ps, 1)

            def tail_item(b, item):
                if item[0] == "out":
                    shared(item, b)
                if item[0] == "gate1":
                    free()
                    gate1(b)
                    reader[0] = (y1_done, n_one(b, 0))
                if item[0] == "gate2":
                    free()
                    gate2(b)
                    reader[0] = (y2_done, n_one(b, 0))

            def attention(b, first, end, prev):
                for g in range(first, end):
                    scores(b, g)
                    if g >= LAG:
                        values(b, g - LAG, prev)
                    h, u = divmod(g, UNITS)
                    for item in beside(h, u):
                        if item[0] == "max":
                            row_max(b, item[1], item[2])
                        else:
                            shared(item, b)
                    for item in tail(h, u) if prev else []:
                        tail_item(b - 1, item)
                    if not prev and (h, u) in SET_UP_AT:
                        set_up(SET_UP_AT[h, u])

            def seam(b, nb, prev):
                for item in SEAM:
                    if item[0] == "qk":
                        shared(("qk", 0, item[1]), nb)
                    if item[0] == "v":
                        v(nb, item[1], prev)
                    if item[0] == "max":
                        row_max(nb, 0, item[1])
                    if item[0] == "shift":
                        shared(("shift", 0, 0), nb)
                    if prev and item[0] == "pv":
                        values(b, item[1], True)

            pe.wait_ge(consts_done, 5)
            pe.wait_ge(vec_loaded, 16 * 8)
            pe.wait_ge(w_lo_done, CK)
            seam(0, 0, False)
            attention(0, 0, HEAD2, False)
            with pe.Fori(0, BATCH - 1) as b:
                reader[0] = (top_row_done, n_shift(b, 4))
                attention(b, HEAD2, STEPS, True)
                seam(b, b + 1, True)
                attention(b + 1, 0, HEAD2, True)
            reader[0] = (top_row_done, n_shift(BATCH - 1, 4))
            attention(BATCH - 1, HEAD2, STEPS, True)
            for g in range(STEPS - LAG, STEPS):
                values(BATCH - 1, g, True)

            def bank_free(i):
                if i >= len(last_banks):
                    pe.wait_ge(out_done, n_out(BATCH - 1, out_i(*TAIL[i - len(last_banks)][1:])))
                elif i < SCORE_BANKS:
                    pe.wait_ge(p_raw_done, n_step(BATCH - 1, STEPS - 1))
                else:
                    free()

            for i, item in enumerate(TAIL):
                if item[0] == "out":
                    out_proj(BATCH - 1, *item[1:], lambda i=i: bank_free(i), last_banks[i % len(last_banks)])
                    reader[0] = (out_done, n_out(BATCH - 1, out_i(*item[1:])))
                else:
                    tail_item(BATCH - 1, item)


_INS = ["x", "L0_conv_W_qkv", "L0_conv_b_qkv", "L0_conv_W_out", "L0_conv_b_out", "L1_conv_w_guide", "L1_conv_w_fuse",
        "L1_conv_bn_gamma", "L1_conv_bn_beta", "L1_conv_bn_mean", "L1_conv_bn_var"]
_OUTS = [((16, 512, 32, 32), "float32")]


def kernel(**inputs):
    import numpy as _np
    import concourse.bacc as _bacc
    from concourse import mybir as _mybir
    from concourse.bass_utils import run_bass_kernel_spmd as _run

    nc = _bacc.Bacc("TRN2", target_bir_lowering=False, num_devices=1, dynamic_dma_scratch_size=4096)
    arrays, args = {}, []
    for name in _INS:
        a = _np.ascontiguousarray(inputs[name])
        arrays[f"in_{name}_dram"] = a
        args.append(nc.dram_tensor(f"in_{name}_dram", a.shape, _mybir.dt.from_np(a.dtype), kind="ExternalInput").ap())
    for i, (shape, dtype) in enumerate(_OUTS):
        dt = _mybir.dt.from_np(_np.dtype(dtype))
        args.append(nc.dram_tensor(f"out_{i}_dram", shape, dt, kind="ExternalOutput").ap())
    attention_block_kernel(nc, *args)
    r = _run(nc, [arrays], core_ids=[0])
    return r.results[0]["out_0_dram"]
```
